# Optimizing a Trainium2 kernel written in Bass

```python
import numpy as np
import jax
import jax.numpy as jnp

def _softmax(x, axis=-1):
    return jax.nn.softmax(x, axis=axis)

def _gelu(x):
    return jax.nn.gelu(x, approximate=True)

def _silu(x):
    return jax.nn.silu(x)

def _sigmoid(x):
    return jax.nn.sigmoid(x)

def _layernorm(x, axis=-1, eps=1e-05):
    m = jnp.mean(x, axis=axis, keepdims=True)
    v = jnp.var(x, axis=axis, keepdims=True)
    return (x - m) / jnp.sqrt(v + eps)

def _scatter_add(tgt, idx, src, axis=0):
    return tgt.at[idx].add(src)

def _segment_sum(src, seg, n):
    return jax.ops.segment_sum(src, seg, n)
kernel_name = 'mk_decoder_preln_d1_seqx_r4_36b8fe'

def setup_inputs(seed: int=0):
    np.random.seed(seed)
    _w = jnp.asarray

    def _rec_inputs():
        import jax
        import jax.numpy as jnp
        _rk = jax.random.key(seed)
        x = -0.0003929 + 0.9999 * jax.random.normal(jax.random.fold_in(_rk, 1), (32, 256, 256), jnp.float32)
        _lenS = 256 - jax.random.randint(jax.random.fold_in(_rk, 7), (32,), 0, max(1, 256 // 4) + 1, jnp.int32)
        _lenS2 = 77 - jax.random.randint(jax.random.fold_in(_rk, 8), (32,), 0, max(1, 77 // 4) + 1, jnp.int32)
        _ctx_768P = jax.random.normal(jax.random.fold_in(_rk, 11), (32, 16, 192), jnp.float32)
        _ctx_768c = jax.random.dirichlet(jax.random.fold_in(_rk, 511), 0.3 * jnp.ones((16,), jnp.float32), (32, 77))
        _ctx_768t = jnp.einsum('bsk,bkd->bsd', _ctx_768c, _ctx_768P)
        _ctx_768t = _ctx_768t * jax.lax.rsqrt(jnp.mean(jnp.square(_ctx_768t)) + 1e-12) * 0.953939
        ctx_768 = 2.09791e-05 + 1.00001 * (_ctx_768t + 0.3 * jax.random.normal(jax.random.fold_in(_rk, 611), (32, 77, 192), jnp.float32))
        return (x, ctx_768)
    x, ctx_768 = _rec_inputs()

    def _L0_attn_setup():
        import jax, jax.numpy as jnp
        import numpy as np
        EPS_RHO = 1e-08
        EPS_DEN = 1e-09

        def _rho_signed_sqrt(x):
            return jnp.sqrt(jax.nn.relu(x) + EPS_RHO) - jnp.sqrt(jax.nn.relu(-x) + EPS_RHO)
        key = jax.random.key(seed)
        ks = jax.random.split(key, 8)
        B, N, C, A = (2, 128, 256, 64)
        s_c = 1.0 / np.sqrt(C)
        s_a = 1.0 / np.sqrt(A)
        return {'X': jax.random.normal(ks[0], (B, N, C), jnp.float32), 'Wq': jax.random.normal(ks[1], (A, C), jnp.float32) * s_c, 'Wk': jax.random.normal(ks[2], (A, C), jnp.float32) * s_c, 'Wphi': jax.random.normal(ks[3], (A,), jnp.float32) * s_a, 'Wy_w': jax.random.normal(ks[4], (C, C), jnp.float32) * s_c, 'Wy_b': jax.random.normal(ks[5], (C,), jnp.float32) * s_c, 'We_w': jax.random.normal(ks[6], (C, A), jnp.float32) * s_a, 'We_b': jax.random.normal(ks[7], (C,), jnp.float32) * s_a}
    _L0_attn_all = _L0_attn_setup()
    _L0_attn_in = {k: v for k, v in _L0_attn_all.items() if k in ('Wq', 'Wk', 'Wphi', 'Wy_w', 'Wy_b', 'We_w', 'We_b')}
    del _L0_attn_all

    def _L0_xattn_setup():
        import jax, jax.numpy as jnp
        import numpy as np
        QUERY_DIM = 256
        KEY_DIM = 192
        NUM_HEADS = 16
        HEAD_DIM = QUERY_DIM // NUM_HEADS
        SCALE = HEAD_DIM ** (-0.5)
        key = jax.random.key(seed)
        ks = jax.random.split(key, 11)
        B, Nq, Nk = (4, 1024, 256)
        s_q = QUERY_DIM ** (-0.5)
        s_k = KEY_DIM ** (-0.5)
        return {'query': jax.random.normal(ks[0], (B, Nq, QUERY_DIM), jnp.float32), 'key': jax.random.normal(ks[1], (B, Nk, KEY_DIM), jnp.float32), 'value': jax.random.normal(ks[2], (B, Nk, KEY_DIM), jnp.float32), 'Wq': jax.random.normal(ks[3], (QUERY_DIM, QUERY_DIM), jnp.float32) * s_q, 'bq': jnp.zeros((QUERY_DIM,), jnp.float32), 'Wk': jax.random.normal(ks[4], (KEY_DIM, QUERY_DIM), jnp.float32) * s_k, 'bk': jnp.zeros((QUERY_DIM,), jnp.float32), 'Wv': jax.random.normal(ks[5], (KEY_DIM, QUERY_DIM), jnp.float32) * s_k, 'bv': jnp.zeros((QUERY_DIM,), jnp.float32), 'Wo': jax.random.normal(ks[6], (QUERY_DIM, QUERY_DIM), jnp.float32) * s_q, 'bo': jnp.zeros((QUERY_DIM,), jnp.float32)}
    _L0_xattn_all = _L0_xattn_setup()
    _L0_xattn_in = {k: v for k, v in _L0_xattn_all.items() if k in ('Wq', 'bq', 'Wk', 'bk', 'Wv', 'bv', 'Wo', 'bo')}
    del _L0_xattn_all

    def _L0_ffn_setup():
        import jax, jax.numpy as jnp
        import numpy as np
        B, S, D, F, E = (4, 1024, 256, 512, 8)
        key = jax.random.key(seed)
        ks = jax.random.split(key, 8)
        x = jax.random.normal(ks[0], (B, S, D), dtype=jnp.float32)
        Wr = jax.random.normal(ks[1], (D, E), dtype=jnp.float32) * 0.02
        br = jnp.zeros((E,), dtype=jnp.float32)
        W1 = jax.random.normal(ks[2], (E, D, F), dtype=jnp.float32) * (1.0 / np.sqrt(D))
        b1 = jnp.zeros((E, F), dtype=jnp.float32)
        W2 = jax.random.normal(ks[3], (E, F, D), dtype=jnp.float32) * (1.0 / np.sqrt(F))
        b2 = jnp.zeros((E, D), dtype=jnp.float32)
        return {'x': x, 'Wr': Wr, 'br': br, 'W1': W1, 'b1': b1, 'W2': W2, 'b2': b2}
    _L0_ffn_all = _L0_ffn_setup()
    _L0_ffn_in = {k: v for k, v in _L0_ffn_all.items() if k in ('Wr', 'br', 'W1', 'b1', 'W2', 'b2')}
    del _L0_ffn_all
    return {'x': x, 'ctx_768': ctx_768, 'L0_attn_Wq': _L0_attn_in['Wq'], 'L0_attn_Wk': _L0_attn_in['Wk'], 'L0_attn_Wphi': _L0_attn_in['Wphi'], 'L0_attn_Wy_w': _L0_attn_in['Wy_w'], 'L0_attn_Wy_b': _L0_attn_in['Wy_b'], 'L0_attn_We_w': _L0_attn_in['We_w'], 'L0_attn_We_b': _L0_attn_in['We_b'], 'L0_xattn_Wq': _L0_xattn_in['Wq'], 'L0_xattn_bq': _L0_xattn_in['bq'], 'L0_xattn_Wk': _L0_xattn_in['Wk'], 'L0_xattn_bk': _L0_xattn_in['bk'], 'L0_xattn_Wv': _L0_xattn_in['Wv'], 'L0_xattn_bv': _L0_xattn_in['bv'], 'L0_xattn_Wo': _L0_xattn_in['Wo'], 'L0_xattn_bo': _L0_xattn_in['bo'], 'L0_ffn_Wr': _L0_ffn_in['Wr'], 'L0_ffn_br': _L0_ffn_in['br'], 'L0_ffn_W1': _L0_ffn_in['W1'], 'L0_ffn_b1': _L0_ffn_in['b1'], 'L0_ffn_W2': _L0_ffn_in['W2'], 'L0_ffn_b2': _L0_ffn_in['b2']}

def reference(x, ctx_768, L0_attn_Wq, L0_attn_Wk, L0_attn_Wphi, L0_attn_Wy_w, L0_attn_Wy_b, L0_attn_We_w, L0_attn_We_b, L0_xattn_Wq, L0_xattn_bq, L0_xattn_Wk, L0_xattn_bk, L0_xattn_Wv, L0_xattn_bv, L0_xattn_Wo, L0_xattn_bo, L0_ffn_Wr, L0_ffn_br, L0_ffn_W1, L0_ffn_b1, L0_ffn_W2, L0_ffn_b2):
    import jax
    import jax.numpy as jnp

    def _L0_attn_ref(X, Wq, Wk, Wphi, Wy_w, Wy_b, We_w, We_b):
        import jax, jax.numpy as jnp
        import numpy as np
        EPS_RHO = 1e-08
        EPS_DEN = 1e-09

        def _rho_signed_sqrt(x):
            return jnp.sqrt(jax.nn.relu(x) + EPS_RHO) - jnp.sqrt(jax.nn.relu(-x) + EPS_RHO)
        q = jnp.einsum('bnc,ac->bna', X, Wq)
        k = jnp.einsum('bnc,ac->bna', X, Wk)
        Vy = jnp.einsum('bnc,dc->bnd', X, Wy_w) + Wy_b
        e = jax.nn.relu(_rho_signed_sqrt(q[:, :, None, :] + k[:, None, :, :]))
        scores = jnp.einsum('bija,a->bij', e, Wphi)
        m = jnp.max(scores, axis=-1, keepdims=True)
        ex = jnp.exp(scores - m)
        denom = jnp.sum(ex, axis=-1)
        part1 = jnp.einsum('bij,bjc->bic', ex, Vy)
        Ew = jnp.einsum('bij,bija->bia', ex, e)
        part2 = jnp.einsum('bia,ca->bic', Ew, We_w) + We_b * denom[..., None]
        return (part1 + part2) / (denom[..., None] + EPS_DEN)

    def _L0_xattn_ref(query, key, value, Wq, bq, Wk, bk, Wv, bv, Wo, bo):
        import jax, jax.numpy as jnp
        import numpy as np
        QUERY_DIM = 256
        KEY_DIM = 192
        NUM_HEADS = 16
        HEAD_DIM = QUERY_DIM // NUM_HEADS
        SCALE = HEAD_DIM ** (-0.5)
        B, Nq, _ = query.shape
        Nk = key.shape[1]
        q = (query @ Wq + bq).reshape(B, Nq, NUM_HEADS, HEAD_DIM).transpose(0, 2, 1, 3)
        k = (key @ Wk + bk).reshape(B, Nk, NUM_HEADS, HEAD_DIM).transpose(0, 2, 1, 3)
        v = (value @ Wv + bv).reshape(B, Nk, NUM_HEADS, HEAD_DIM).transpose(0, 2, 1, 3)
        attn = jnp.einsum('bhqd,bhkd->bhqk', q, k) * SCALE
        attn = jax.nn.softmax(attn, axis=-1)
        out = jnp.einsum('bhqk,bhkd->bhqd', attn, v)
        out = out.transpose(0, 2, 1, 3).reshape(B, Nq, QUERY_DIM)
        return out @ Wo + bo

    def _L0_ffn_ref(x, Wr, br, W1, b1, W2, b2):
        import jax, jax.numpy as jnp
        import numpy as np
        B, S, D, F, E = (4, 1024, 256, 512, 8)
        logits = jnp.einsum('bsd,de->bse', x, Wr) + br
        probs = jax.nn.softmax(logits, axis=-1)
        expert_weights = jnp.max(probs, axis=-1)
        expert_indices = jnp.argmax(probs, axis=-1)
        num_experts = W1.shape[0]
        out = jnp.zeros_like(x)
        for e in range(num_experts):
            h = jax.nn.gelu(jnp.einsum('bsd,df->bsf', x, W1[e]) + b1[e], approximate=False)
            y = jnp.einsum('bsf,fd->bsd', h, W2[e]) + b2[e]
            out = jnp.where((expert_indices == e)[..., None], y, out)
        return out * expert_weights[..., None]
    x = x + _L0_attn_ref(_layernorm(x, axis=-1), L0_attn_Wq, L0_attn_Wk, L0_attn_Wphi, L0_attn_Wy_w, L0_attn_Wy_b, L0_attn_We_w, L0_attn_We_b)
    x = x + _L0_xattn_ref(_layernorm(x, axis=-1), ctx_768, ctx_768, L0_xattn_Wq, L0_xattn_bq, L0_xattn_Wk, L0_xattn_bk, L0_xattn_Wv, L0_xattn_bv, L0_xattn_Wo, L0_xattn_bo)
    x = x + _L0_ffn_ref(_layernorm(x, axis=-1), L0_ffn_Wr, L0_ffn_br, L0_ffn_W1, L0_ffn_b1, L0_ffn_W2, L0_ffn_b2)
    return x

_drawn_inputs = setup_inputs


def setup_inputs(seed=0):
    import zlib

    import numpy as np

    out = dict(_drawn_inputs(seed))
    spreads = {'L0_xattn_bq': (0.0, 0.323),
     'L0_xattn_bk': (0.0, 0.8),
     'L0_xattn_bv': (0.0, 0.1),
     'L0_xattn_bo': (0.0, 0.1),
     'L0_ffn_br': (0.0, 0.1),
     'L0_ffn_b1': (0.0, 0.768),
     'L0_ffn_b2': (0.0, 0.525)}
    factors = {}
    for name, (base, spread) in spreads.items():
        noise = np.random.default_rng([zlib.crc32(name.encode()), seed]).standard_normal(out[name].shape)
        drawn = base * np.exp(spread * noise) if base else spread * noise
        out[name] = jnp.asarray(drawn.astype(out[name].dtype))
    for name, factor in factors.items():
        out[name] = (out[name] * factor).astype(out[name].dtype)
    return out
```

```python
import concourse.bass as bass
from concourse import mybir
from contextlib import ExitStack

F32 = mybir.dt.float32
BF16 = mybir.dt.bfloat16
ALU = mybir.AluOpType
ACT = mybir.ActivationFunctionType
AX = mybir.AxisListType
I32 = mybir.dt.int32

B, N, C, A = 32, 256, 256, 64
CD, NK, H, D = 192, 77, 16, 16
E, F = 8, 512
P = 128
UNITS = B * N // P
PAIRS = P // 2
CHUNK = 8
STEPS = PAIRS // CHUNK
GROUPS = 4
SIDE = PAIRS // GROUPS
KC = C // P
CC = CD // 2
LAG = 2
REGION = B * N + P
TILES = B * N // P + E
ROW = C + 4
AT_ID, AT_WEIGHT, AT_MEAN, AT_SCALE = range(C, C + 4)
ROUTE = 16 + B * N // P + TILES + 1
NO_ROW = 2.0 * B * N
EPS_RHO, EPS_DEN, EPS_LN = 1e-8, 1e-9, 1e-5
ON_POOL, ON_ACT = (2, 6), (1, 4, 7)
ON_DVE = tuple(p for p in range(CHUNK) if p not in ON_POOL + ON_ACT)


def wait(eng, sem, n):
    if isinstance(n, int) and n <= 0:
        return
    eng.wait_ge(sem, n)


def is_unit(n):
    return not isinstance(n, int) or 0 <= n < UNITS


def is_tile(t):
    return not isinstance(t, int) or 0 <= t < TILES


def is_batch(n):
    return not isinstance(n, int) or 0 <= n < B


def decoder(nc, x, ctxT, wq, wk, wphi, wy, wy_b, we, we_b, xwq, xbq, xwk, xbk, xwv, xbv, xwo, xbo,
            wr, br, w1, w2, b12, ident_h, tri_h, selw_h, selb_h, headmask_h, route_h, out):
    rows = x.rearrange("b (u p) c -> p (b u) c", p=P)
    out_rows = out.rearrange("b n c -> (b n) c")
    regions = nc.dram_tensor("regions", (E * REGION + P, ROW), F32, kind="Internal").ap()

    with ExitStack() as ctx:
        def sb(name, shape, dt=F32):
            return ctx.enter_context(nc.sbuf_tensor(name, shape, dt))

        def sem(name):
            return ctx.enter_context(nc.semaphore(name))

        bank = [ctx.enter_context(nc.psum_tensor(f"bank{i}", [P, 512], F32)) for i in range(8)]
        score_bank, weight_bank = bank[0:2], bank[2:4]
        xa, xb, sa, sb_ = bank[4], bank[5], bank[6], bank[7]

        e = sb("e", [P, 2, STEPS, CHUNK, N])
        ident = sb("ident", [P, P])
        eps_rho = sb("eps_rho", [P, 1])
        eps_ln = sb("eps_ln", [P, 1])
        phi = sb("phi", [P, 1])
        selw = sb("selw", [P, SIDE, 32])
        selb = sb("selb", [3 * 32, SIDE, P], BF16)
        wq_s = sb("wq_s", [P, KC, P])
        wk_s = sb("wk_s", [P, KC, P])
        wy_s = sb("wy_s", [P, KC, C])
        we_s = sb("we_s", [P, C + 1])
        vbias = sb("vbias", [P, C])
        minus_rho = sb("minus_rho", [A, P])
        xin = sb("xin", [P, 2, C])
        xnT = sb("xnT", [P, KC, N])
        st1 = sb("st1", [P, 2, 6])
        mv1 = sb("mv1", [P, 2, 2])
        sd1 = sb("sd1", [P, 2])
        rs1 = sb("rs1", [P, 2])
        k2 = sb("k2", [P, 2, N])
        q2 = sb("q2", [P, 2, 2, GROUPS, SIDE])
        vy = sb("vy", [P, 2, 2, C + 1])
        nmax = sb("nmax", [P, 1])
        ex = sb("ex", [P, N])
        rem = sb("rem", [P, N])
        parts = sb("parts", [P, 3, N], BF16)
        g3 = sb("g3", [3 * 32, 2, GROUPS, N], BF16)
        exT = sb("exT", [P, 2, P])
        ew = sb("ew", [P, 2, GROUPS, SIDE])
        ew2 = sb("ew2", [P, GROUPS, 2, SIDE])
        xres = sb("xres", [P, 2, C])
        den = sb("den", [P, 1])
        rden = sb("rden", [P, 1])
        x1 = sb("x1", [P, C])
        xwq_s = sb("xwq_s", [P, KC, C])
        xwk_s = sb("xwk_s", [CC, 2, C])
        xwv_s = sb("xwv_s", [CC, 2, C])
        xwo_s = sb("xwo_s", [P, KC, C])
        xbq_s = sb("xbq_s", [P, KC])
        xbk_s = sb("xbk_s", [P, KC])
        xbv_s = sb("xbv_s", [NK, C])
        xbo_s = sb("xbo_s", [P, C])
        headmask = sb("headmask", [P, H // 2])
        cT = sb("cT", [CC, 2, NK])
        kT = sb("kT", [P, KC, NK])
        kbd = sb("kbd", [P, KC, H // 2, NK])
        vx = sb("vx", [NK, H, D + 1])
        st2 = sb("st2", [P, 6])
        mv2 = sb("mv2", [P, 2])
        sd2 = sb("sd2", [P, 1])
        rs2 = sb("rs2", [P, 1])
        xn2 = sb("xn2", [P, C])
        xn2T = sb("xn2T", [P, KC, P])
        qT = sb("qT", [P, KC, P])
        hmax = sb("hmax", [P, H])
        pr = sb("pr", [P, H, NK])
        pT = sb("pT", [NK, H, P])
        hden = sb("hden", [P, H])
        att = sb("att", [P, H, D])
        attT = sb("attT", [P, KC, P])
        x1b = sb("x1b", [P, C])
        pay = sb("pay", [P, 2, ROW])
        st3 = sb("st3", [P, 6])
        sd3 = sb("sd3", [P, 1])
        xn3 = sb("xn3", [P, C])
        xn3T = sb("xn3T", [P, KC, P])
        wr_s = sb("wr_s", [P, KC, E])
        br_s = sb("br_s", [P, E])
        tri = sb("tri", [P, 2, P])
        route = sb("route", [P, ROUTE])
        tie, base0 = route[:, 0:E], route[:, E:2 * E]
        full, tile_no = route[:, 16:16 + UNITS], route[:, 16 + UNITS:ROUTE - 1]
        row_id = route[:, ROUTE - 1:ROUTE]
        lg = sb("lg", [P, E])
        nlmax = sb("nlmax", [P, 1])
        key = sb("key", [P, E])
        kmax = sb("kmax", [P, 1])
        oh = sb("oh", [P, E])
        base = sb("base", [P, E])
        rank = sb("rank", [P, E])
        pos = sb("pos", [P, 1])
        posi = sb("posi", [P, 1], I32)
        els = sb("els", [P, E])
        sume = sb("sume", [P, 1])

        s_const = sem("consts_loaded")
        s_setup = sem("setup_vector")
        s_vb_ps = sem("vbias_psum")
        s_x_in = sem("x_loaded")
        s_ctx_in = sem("context_loaded")
        s_res_in = sem("residual_loaded")
        s_st1 = sem("ln1_stats")
        s_mv1 = sem("ln1_variance")
        s_sd1 = sem("ln1_deviation")
        s_rs1 = sem("ln1_scale")
        s_xn1 = sem("ln1_rows")
        s_xnT_ps = sem("xnT_in_psum")
        s_xnT = sem("xnT_ready")
        s_q_ps = sem("q_in_psum")
        s_q = sem("q_ready")
        s_k_ps = sem("k_in_psum")
        s_k = sem("k_ready")
        s_vy_ps = sem("vy_in_psum")
        s_vy = sem("vy_ready")
        s_relu_dve = sem("relu_vector")
        s_relu_act = sem("relu_scalar")
        s_relu_pool = sem("relu_pool")
        s_sqrt = sem("sqrt_done")
        s_scores = sem("scores_ready")
        s_nmax = sem("negmax_ready")
        s_ex = sem("exp_ready")
        s_hi = sem("hi_ready")
        s_r1 = sem("rest1_ready")
        s_mid = sem("mid_ready")
        s_split = sem("split_ready")
        s_g3 = sem("g3_loaded")
        s_wb = sem("weights_in_psum")
        s_summed = sem("pairs_summed")
        s_exT_ps = sem("exT_in_psum")
        s_exT = sem("exT_ready")
        s_ew2 = sem("ew2_ready")
        s_o_ps = sem("o_in_psum")
        s_den = sem("den_ready")
        s_rden = sem("rden_ready")
        s_x1 = sem("x1_ready")
        s_st2 = sem("ln2_stats")
        s_mv2 = sem("ln2_variance")
        s_sd2 = sem("ln2_deviation")
        s_rs2 = sem("ln2_scale")
        s_xn2 = sem("ln2_rows")
        s_xn2T_ps = sem("xn2T_in_psum")
        s_xn2T = sem("xn2T_ready")
        s_qT_ps = sem("qT_in_psum")
        s_qT = sem("qT_ready")
        s_kv_ps = sem("kv_in_psum")
        s_kT = sem("kT_ready")
        s_vx = sem("vx_ready")
        s_kbd = sem("kbd_ready")
        s_xs_ps = sem("xscores_in_psum")
        s_hmax = sem("head_max_ready")
        s_sub = sem("xscores_shifted")
        s_pr = sem("probs_ready")
        s_pT_ps = sem("pT_in_psum")
        s_pT = sem("pT_ready")
        s_pv_ps = sem("pv_in_psum")
        s_hden = sem("head_den_ready")
        s_att = sem("att_ready")
        s_attT_ps = sem("attT_in_psum")
        s_attT = sem("attT_ready")
        s_x1b = sem("x1_with_bias")
        s_y_ps = sem("xattn_out_in_psum")
        s_x2 = sem("x2_ready")
        s_st3 = sem("ln3_stats")
        s_mv3 = sem("ln3_variance")
        s_sd3 = sem("ln3_deviation")
        s_rs3 = sem("ln3_scale")
        s_xn3 = sem("ln3_rows")
        s_xn3T_ps = sem("xn3T_in_psum")
        s_xn3T = sem("xn3T_ready")
        s_lg_ps = sem("logits_in_psum")
        s_lg = sem("logits_ready")
        s_lmax = sem("logit_max_ready")
        s_lsub = sem("logits_shifted")
        s_key = sem("key_ready")
        s_kmax = sem("key_max_ready")
        s_oh = sem("onehot_ready")
        s_rank_ps = sem("rank_in_psum")
        s_rank = sem("rank_ready")
        s_base = sem("base_moved")
        s_pos = sem("position_ready")
        s_posi = sem("position_integer")
        s_els = sem("logit_exp_ready")
        s_wt = sem("weight_ready")
        s_id = sem("row_number_written")
        s_idn = sem("row_number_moved")
        s_scat = sem("rows_scattered")

        stage = e[:].rearrange("p u j q n -> p (u j q n)")
        consts = [
            (ident[:], ident_h), (phi[0:A, :], wphi), (phi[A:P, :], wphi), (stage[:, 0:512], selw_h),
            (stage[0:96, 512:2560], selb_h), (wq_s[:, :, 0:A], wq), (wq_s[:, :, A:P], wq), (wk_s[:, :, 0:A], wk),
            (wk_s[:, :, A:P], wk), (wy_s[:], wy), (we_s[0:A, 0:C], we), (we_s[A:P, 0:C], we),
            (stage[:, 2560:2816], wy_b), (stage[:, 2816:3072], we_b), (xwq_s[:], xwq), (xwk_s[:], xwk), (xwv_s[:], xwv),
            (xwo_s[:], xwo), (xbq_s[:], xbq), (xbk_s[:], xbk), (xbv_s[:], xbv), (xbo_s[:], xbo),
            (headmask[:], headmask_h), (wr_s[:], wr), (br_s[:], br), (tri[:], tri_h), (route[:], route_h),
        ]
        SETUP = 12
        block = ctx.enter_context(nc.Block())

        s_taken = sem("waits_taken")

        def take_waits(eng):
            eng.sem_inc(s_taken, 1)

        def slots(eng, slot):
            for v in range(-1, 8):
                slot(v, v // 2, v % 4)
            with eng.Fori(2, UNITS // 4 - 1) as i:
                for c in range(4):
                    slot(4 * i + c, 2 * i + c // 2, c)
            for v in range(UNITS - 4, UNITS + 5):
                slot(v, v // 2, v % 4)

        flat = e[:].rearrange("p u j q n -> p (u j q n)")
        HALF = STEPS * CHUNK * N
        taken = [HALF]

        def room(cols, dt=F32):
            words = cols if dt != BF16 else cols // 2
            at, taken[0] = taken[0], taken[0] + words
            v = flat[:, at:at + words]
            return v if dt == F32 else v.bitcast(dt)

        FC = F // P
        w1_s = flat[:, 0:E * KC * F].rearrange("p (e k f) -> p e k f", e=E, k=KC)
        w2_s = flat[:, E * KC * F:E * (KC * F + FC * C)].rearrange("p (e k c) -> p e k c", e=E, k=FC)
        BIAS = E * (F + C)
        tin = room(4 * ROW).rearrange("p (b r) -> p b r", b=4)
        xnb = room(2 * C).rearrange("p (b c) -> p b c", b=2)
        xnbT = room(2 * C).rearrange("p (b k n) -> p b k n", b=2, k=KC)
        hid = room(2 * F).rearrange("p (b f) -> p b f", b=2)
        hidT = room(2 * F).rearrange("p (b k n) -> p b k n", b=2, k=FC)
        yout = room(2 * C).rearrange("p (b c) -> p b c", b=2)
        rowi = room(2, I32)
        brows = room(BIAS, BF16)[0:3, :]
        bstage = room(BIAS // P)
        brem = room(BIAS // P)
        bsplit = room(3 * BIAS // P + BIAS // P % 2, BF16)[:, 0:3 * BIAS // P].rearrange("p (t n) -> p t n", t=3)
        ones3 = room(P, BF16)[0:3, :]
        fill = room(ROW)
        cnt, ntile, tend, tword = room(E), room(E), room(E), room(E)
        above = room(E * UNITS).rearrange("p (e k) -> p e k", e=E)
        past = room(TILES * E).rearrange("p (t e) -> p t e", e=E)
        past2 = room(TILES * E).rearrange("p (t e) -> p t e", e=E)
        texp, toff, toff2 = room(TILES), room(TILES), room(TILES)
        texp_i, toff_i = room(TILES, I32), room(TILES, I32)
        base_i = room(E, I32)
        assert taken[0] <= 2 * HALF
        hid_bank, row_bank, y_bank, hidT_bank = bank[1:3], bank[3:5], bank[5:7], bank[0]

        s_w_in = sem("expert_weights_loaded")
        s_b_in = sem("biases_loaded")
        s_b_hi = sem("bias_hi")
        s_b_r1 = sem("bias_rest1")
        s_b_mid = sem("bias_mid")
        s_b_lo = sem("bias_lo")
        s_b_rows = sem("bias_rows_loaded")
        s_plan = sem("plan_steps")
        s_fill = sem("filling_stored")
        s_tin = [sem(f"tile_loaded{i}") for i in range(4)]
        s_xnb = sem("tile_rows_normal")
        s_xT_ps = sem("tile_transposed_in_psum")
        s_xT = sem("tile_transposed")
        s_h_ps = sem("hidden_in_psum")
        s_h = sem("hidden_ready")
        s_hT_ps = sem("hiddenT_in_psum")
        s_hT = sem("hiddenT_ready")
        s_yt_ps = sem("tile_out_in_psum")
        s_rowi = sem("row_numbers_integer")
        s_yt = sem("tile_out_ready")
        s_out = [sem(f"tile_scattered{i}") for i in range(2)]
        PLAN = 15

        def tiles(eng, step, before):
            for t in range(-before, 4):
                step(t, t % 4)
            with eng.Fori(1, TILES // 4 - 1) as i:
                for c in range(4):
                    step(4 * i + c, c)
            for t in range(TILES - 4, TILES + 2):
                step(t, t % 4)

        def moe_loads(sp):
            sp.wait_ge(s_summed, 32 * (UNITS - 1))
            for i in range(E):
                sp.dma_start(w1_s[:, i, :, :], w1[:, i, :, :]).then_inc(s_w_in, 16)
                sp.dma_start(w2_s[:, i, :, :], w2[:, i, :, :]).then_inc(s_w_in, 16)
            sp.wait_ge(s_summed, 32 * UNITS)
            sp.dma_start(bstage, b12).then_inc(s_b_in, 16)
            sp.wait_ge(s_b_lo, 1)
            for i in range(3):
                sp.dma_start(brows[i:i + 1, :], bsplit[:, i, :]).then_inc(s_b_rows, 16)
            sp.wait_ge(s_plan, PLAN)
            sp.wait_ge(s_scat, 16 * UNITS)
            for i in range(E):
                end = sp.value_load(base_i[0:1, i:i + 1], min_val=i * REGION, max_val=i * REGION + B * N)
                sp.dma_start(regions[bass.ds(end, P), :], fill).then_inc(s_fill, 16)
            sp.dma_start(regions[E * REGION:E * REGION + P, :], fill).then_inc(s_fill, 16)
            sp.wait_ge(s_fill, 16 * (E + 1))

            def load(t, c):
                n = t + 3
                if not is_tile(n):
                    return
                at = sp.value_load(toff_i[0:1, bass.ds(n, 1)], min_val=0, max_val=E * REGION)
                wait(sp, s_yt, n - 3)
                take_waits(sp)
                sp.dma_start(tin[:, (c + 3) % 4, :], regions[bass.ds(at, P), :]).then_inc(s_tin[(c + 3) % 4], 16)

            tiles(sp, load, 3)

        def moe_scatter(pool):
            last_row = pool.snap(pool.to_reg(B * N - 1))

            def store(t, c):
                n = t - 1
                if not is_tile(n):
                    return
                par = (c - 1) % 2
                pool.wait_ge(s_yt, n + 1)
                pool.wait_ge(s_rowi, n + 1)
                take_waits(pool)
                nc.gpsimd.indirect_dma_start(
                    out=out_rows, out_offset=bass.IndirectOffsetOnAxis(ap=rowi[:, par:par + 1], axis=0),
                        in_=yout[:, par, :], in_offset=None, bounds_check=last_row, oob_is_err=False
                ).then_inc(s_out[par], 16)

            tiles(pool, store, 0)
            for par in range(2):
                pool.wait_ge(s_out[par], 16 * TILES // 2)

        def moe_gelu(act):
            act.wait_ge(s_summed, 32 * UNITS)

            def step(t, c):
                par, last = c % 2, (c + 1) % 2
                if is_tile(t - 1):
                    act.wait_ge(s_hT_ps, t)
                    wait(act, s_yt_ps, t - 2)
                    nc.scalar.activation(hidT[:, last, :, :], hidT_bank[:, :].rearrange("p (k n) -> p k n", k=FC),
                                         ACT.Copy).then_inc(s_hT, 1)
                if is_tile(t):
                    act.wait_ge(s_h_ps, t + 1)
                    wait(act, s_hT_ps, t - 1)
                    nc.scalar.activation(hid[:, par, :], hid_bank[par][:, :], ACT.Gelu).then_inc(s_h, 1)

            tiles(act, step, 0)

        def moe_matmuls(pe):
            pe.wait_ge(s_w_in, 16 * 2 * E)
            pe.wait_ge(s_b_rows, 48)
            pe.wait_ge(s_plan, PLAN)
            pe.wait_ge(s_x2, UNITS)
            pe.wait_ge(s_base, UNITS)
            pe.wait_ge(s_ex, UNITS)

            def step(t, c):
                par, last = c % 2, (c + 1) % 2
                if is_tile(t - 1):
                    pe.wait_ge(s_h, t)
                    wait(pe, s_hT, t - 1)
                    for k in range(FC):
                        op = nc.tensor.transpose(hidT_bank[:, k * P:(k + 1) * P], hid[:, last, k * P:(k + 1) * P],
                                                 ident[:])
                    op.then_inc(s_hT_ps, 1)
                if is_tile(t):
                    ex_t = pe.value_load(texp_i[0:1, bass.ds(t, 1)], min_val=0, max_val=E - 1)
                    pe.wait_ge(s_xT, t + 1)
                    wait(pe, s_h, t - 1)
                    nc.tensor.matmul(hid_bank[par][:, :], ones3, brows[:, bass.ds(ex_t * F, F)],
                                     start=True, stop=False)
                    for k in range(KC):
                        op = nc.tensor.matmul(hid_bank[par][:, :], xnbT[:, par, k, :],
                                              flat[:, bass.ds(ex_t * (KC * F) + k * F, F)],
                                              start=False, stop=(k == KC - 1))
                    op.then_inc(s_h_ps, 1)
                if is_tile(t + 1):
                    pe.wait_ge(s_xnb, t + 2)
                    wait(pe, s_xT, t)
                    for k in range(KC):
                        op = nc.tensor.transpose(row_bank[last][:, k * P:(k + 1) * P],
                                                 xnb[:, last, k * P:(k + 1) * P], ident[:])
                    op.then_inc(s_xT_ps, 1)
                if is_tile(t - 1):
                    ex_l = pe.value_load(texp_i[0:1, bass.ds(t - 1, 1)], min_val=0, max_val=E - 1)
                    pe.wait_ge(s_hT, t)
                    wait(pe, s_yt, t - 2)
                    nc.tensor.matmul(y_bank[last][:, 0:C], ones3, brows[:, bass.ds(ex_l * C + E * F, C)],
                                     start=True, stop=False)
                    for k in range(FC):
                        op = nc.tensor.matmul(y_bank[last][:, 0:C], hidT[:, last, k, :],
                                              flat[:, bass.ds(ex_l * (FC * C) + (E * KC * F + k * C), C)],
                                              start=False, stop=(k == FC - 1))
                    op.then_inc(s_yt_ps, 1)

            tiles(pe, step, 1)

        def moe_vector(dve):
            plan = [0]

            def planned(op):
                plan[0] += 1
                op.then_inc(s_plan, 1)
                dve.wait_ge(s_plan, plan[0])

            dve.wait_ge(s_summed, 32 * UNITS)
            dve.wait_ge(s_base, UNITS)
            planned(nc.vector.tensor_tensor(cnt, base[:], base0, ALU.subtract))
            planned(nc.vector.tensor_tensor(above, cnt.unsqueeze(2).to_broadcast([P, E, UNITS]),
                                            full.unsqueeze(1).to_broadcast([P, E, UNITS]), ALU.is_gt))
            planned(nc.vector.tensor_reduce(ntile, above, AX.X, ALU.add))
            planned(nc.vector.tensor_tensor_scan(tend, tri[:, 1, 0:E], ntile, 0.0, ALU.mult, ALU.add))
            planned(nc.vector.tensor_tensor(past, tend.unsqueeze(1).to_broadcast([P, TILES, E]),
                                            tile_no.unsqueeze(2).to_broadcast([P, TILES, E]), ALU.is_le))
            planned(nc.vector.tensor_reduce(texp, past, AX.X, ALU.add))
            planned(nc.vector.tensor_scalar(tword, ntile, -float(P), float(REGION), ALU.mult, ALU.add))
            planned(nc.vector.tensor_tensor(past2, past, tword.unsqueeze(1).to_broadcast([P, TILES, E]), ALU.mult))
            planned(nc.vector.tensor_reduce(toff, past2, AX.X, ALU.add))
            planned(nc.vector.scalar_tensor_tensor(toff2, tile_no, float(P), toff, ALU.mult, ALU.add))
            planned(nc.vector.tensor_scalar(toff_i, toff2, float(E * REGION), None, ALU.min))
            planned(nc.vector.tensor_scalar(texp_i, texp, float(E - 1), None, ALU.min))
            planned(nc.vector.tensor_copy(base_i, base[:]))
            planned(nc.vector.memset(fill, 0.0))
            planned(nc.vector.memset(fill[:, AT_ID:AT_ID + 1], NO_ROW))
            assert plan[0] == PLAN
            nc.vector.memset(ones3, 1.0)
            dve.wait_ge(s_b_in, 16)
            nc.vector.tensor_copy(bsplit[:, 0, :], bstage).then_inc(s_b_hi, 1)
            dve.wait_ge(s_b_hi, 1)
            nc.vector.tensor_tensor(brem, bstage, bsplit[:, 0, :], ALU.subtract).then_inc(s_b_r1, 1)
            dve.wait_ge(s_b_r1, 1)
            nc.vector.tensor_copy(bsplit[:, 1, :], brem).then_inc(s_b_mid, 1)
            dve.wait_ge(s_b_mid, 1)
            nc.vector.tensor_tensor(bsplit[:, 2, :], brem, bsplit[:, 1, :], ALU.subtract).then_inc(s_b_lo, 1)

            def step(t, c):
                par, last = c % 2, (c + 1) % 2
                if is_tile(t + 1):
                    dve.wait_ge(s_xT_ps, t + 2)
                    wait(dve, s_h_ps, t)
                    nc.vector.tensor_copy(xnbT[:, last, :, :], row_bank[last][:, 0:C].rearrange(
                        "p (k n) -> p k n", k=KC)).then_inc(s_xT, 1)
                if is_tile(t + 2):
                    n, slot4 = t + 2, (c + 2) % 4
                    dve.wait_ge(s_tin[slot4], load_count(n, slot4))
                    wait(dve, s_xT_ps, n - 1)
                    nc.vector.tensor_scalar(xnb[:, par, :], tin[:, slot4, 0:C],
                                            tin[:, slot4, AT_MEAN:AT_MEAN + 1], tin[:, slot4, AT_SCALE:AT_SCALE + 1],
                                            ALU.subtract, ALU.mult).then_inc(s_xnb, 1)
                if is_tile(t - 1):
                    n, slot4 = t - 1, (c + 3) % 4
                    wait(dve, s_out[last], 8 * (n - last))
                    nc.vector.tensor_copy(rowi[:, last:last + 1], tin[:, slot4, AT_ID:AT_ID + 1]).then_inc(s_rowi, 1)
                    dve.wait_ge(s_yt_ps, n + 1)
                    nc.vector.scalar_tensor_tensor(yout[:, last, :], y_bank[last][:, 0:C],
                                                   tin[:, slot4, AT_WEIGHT:AT_WEIGHT + 1], tin[:, slot4, 0:C],
                                                   ALU.mult, ALU.add).then_inc(s_yt, 1)

            tiles(dve, step, 2)

        def load_count(n, slot4):
            return 16 * ((n - slot4) // 4 + 1) if isinstance(n, int) else (n - slot4) * 4 + 16

        @block.sync
        def _(sp):
            for dst, src in consts:
                sp.dma_start(dst, src).then_inc(s_const, 16)

            def slot(v, b, c):
                odd, last = c % 2, (c + 1) % 2
                n = v - 1
                if is_unit(n):
                    wait(sp, s_split, n + 1)
                    take_waits(sp)
                    wait(sp, s_summed, 32 * (n - 1))
                    for part in range(3):
                        for g in range(GROUPS):
                            sp.dma_start(g3[32 * part:32 * part + 32, last, g, :],
                                         parts[32 * g:32 * g + 32, part, :]).then_inc(s_g3, 16)
                    wait(sp, s_x1, n - 1)
                    take_waits(sp)
                    sp.dma_start(xres[:, last:last + 1, :], rows[:, bass.ds(n, 1), :]).then_inc(s_res_in, 16)
                if not odd and is_batch(b + 1):
                    wait(sp, s_xnT_ps, b + 1)
                    take_waits(sp)
                    sp.dma_start(xin[:], rows[:, bass.ds(v + 2, 2), :]).then_inc(s_x_in, 16)
                if odd and is_batch(b):
                    wait(sp, s_kv_ps, b)
                    take_waits(sp)
                    sp.dma_start(cT[:], ctxT[:, bass.ds(b, 1), :, :]).then_inc(s_ctx_in, 16)

            sp.dma_start(xin[:], rows[:, 0:2, :]).then_inc(s_x_in, 16)
            slots(sp, slot)
            moe_loads(sp)

        def pair_ap(v_par, j, p):
            return e[:, v_par, j, p, :]

        def query(b_par, u, j, p):
            s = 2 * j + p // GROUPS
            return q2[:, b_par, u, p % GROUPS, s:s + 1]

        def ahead(v, b, c, step):
            if step + 1 < STEPS:
                return v, b, c, step + 1
            return v + 1, (b + c % 2), (c + 1) % 4, 0

        def wait_relu(eng, v, b, j):
            if j == 0:
                wait(eng, s_k, b + 1)
                wait(eng, s_q, 2 * (b + 1))
            wait(eng, s_summed, 32 * (v - 2) + 4 * j + 4)

        @block.gpsimd
        def _(pool):
            pool.wait_ge(s_const, 16 * len(consts))
            pool.wait_ge(s_setup, SETUP)

            def slot(v, b, c):
                for step in range(STEPS):
                    vv, bb, cc, j = ahead(v, b, c, step)
                    if is_unit(vv):
                        wait_relu(pool, vv, bb, j)
                        take_waits(pool)
                        for p in ON_POOL:
                            op = nc.gpsimd.tensor_scalar(
                                pair_ap(cc % 2, j, p), k2[:, cc // 2, :], query(cc // 2, cc % 2, j, p), 0.0,
                                ALU.add, ALU.max)
                        op.then_inc(s_relu_pool, 1)
                    if step == 4 and c % 2 == 0 and is_batch(b - 1):
                        wait(pool, s_kT, 2 * b)
                        wait(pool, s_xs_ps, 4 * (v - 2))
                        for k in range(KC):
                            op = nc.gpsimd.tensor_tensor(
                                kbd[:, k, :, :], kT[:, k, :].unsqueeze(1).to_broadcast([P, H // 2, NK]),
                                headmask[:, :].unsqueeze(2).to_broadcast([P, H // 2, NK]), ALU.mult)
                        op.then_inc(s_kbd, 1)
                    if step == 6 and is_unit(v - 2):
                        pool.wait_ge(s_x1, v - 1)
                        wait(pool, s_x2, v - 2)
                        nc.gpsimd.tensor_tensor(x1b[:], x1[:], xbo_s[:], ALU.add).then_inc(s_x1b, 1)
                    if step == 2 and is_unit(v - 5):
                        row = pay[:, 1 - c % 2, :]
                        wait(pool, s_idn, v - 5)
                        pool.wait_ge(s_x2, v - 4)
                        take_waits(pool)
                        nc.gpsimd.tensor_copy(row[:, AT_ID:AT_ID + 1], row_id).then_inc(s_id, 1)
                        pool.wait_ge(s_id, v - 4)
                        pool.wait_ge(s_wt, v - 4)
                        pool.wait_ge(s_posi, v - 4)
                        take_waits(pool)
                        nc.gpsimd.tensor_scalar(row_id, row_id, float(P), None, ALU.add).then_inc(s_idn, 1)
                        nc.gpsimd.indirect_dma_start(
                            out=regions, out_offset=bass.IndirectOffsetOnAxis(ap=posi[:, 0:1], axis=0),
                            in_=row, in_offset=None).then_inc(s_scat, 16)

            slots(pool, slot)
            moe_scatter(pool)

        @block.scalar
        def _(act):
            act.wait_ge(s_const, 16 * len(consts))
            act.wait_ge(s_setup, SETUP)

            def slot(v, b, c):
                odd, last, pb = c % 2, (c + 1) % 2, c // 2
                for step in range(STEPS):
                    if is_unit(v):
                        wait(act, s_relu_dve, 8 * v + step + 1)
                        wait(act, s_relu_pool, 8 * v + step + 1)
                        wait(act, s_relu_act, 8 * v + step + 1)
                        ej = e[:, odd, step, :, :]
                        nc.scalar.activation(ej, ej, ACT.Sqrt, bias=eps_rho[:]).then_inc(s_sqrt, 1)
                    background(v, b, c, step)
                    vv, bb, cc, j = ahead(v, b, c, step)
                    if is_unit(vv):
                        wait_relu(act, vv, bb, j)
                        for p in ON_ACT:
                            op = nc.scalar.activation(pair_ap(cc % 2, j, p), k2[:, cc // 2, :], ACT.Relu,
                                                      bias=query(cc // 2, cc % 2, j, p))
                        op.then_inc(s_relu_act, 1)
                    if step == 4 and is_unit(v - 2):
                        act.wait_ge(s_mv2, v - 1)
                        wait(act, s_rs2, v - 2)
                        nc.scalar.activation(sd2[:], mv2[:, 1:2], ACT.Sqrt, bias=eps_ln[:]).then_inc(s_sd2, 1)
                    if step == 6 and is_unit(v - 3):
                        act.wait_ge(s_mv3, v - 2)
                        wait(act, s_rs3, v - 3)
                        nc.scalar.activation(sd3[:], pay[:, 1 - c % 2, AT_SCALE:AT_SCALE + 1], ACT.Sqrt,
                                             bias=eps_ln[:]).then_inc(s_sd3, 1)

            def background(v, b, c, step):
                odd, last, pb = c % 2, (c + 1) % 2, c // 2
                nb = (pb + odd) % 2
                if step == 0:
                    if odd and is_batch(b + 1):
                        act.wait_ge(s_mv1, 2 * (b + 2))
                        wait(act, s_rs1, b + 1)
                        nc.scalar.activation(sd1[:], mv1[:, :, 1], ACT.Sqrt, bias=eps_ln[:]).then_inc(s_sd1, 1)
                    if is_unit(v - 1):
                        act.wait_ge(s_nmax, v)
                        wait(act, s_exT_ps, v - 1)
                        wait(act, s_split, v - 1)
                        nc.scalar.activation(ex[:], score_bank[last][:, 0:N], ACT.Exp, bias=nmax[:]).then_inc(s_ex, 1)
                    if is_unit(v - 5):
                        act.wait_ge(s_lsub, v - 4)
                        wait(act, s_wt, v - 5)
                        nc.scalar.activation(els[:], lg[:], ACT.Exp, accum_out=sume[:]).then_inc(s_els, 1)
                    if is_unit(v - 3):
                        act.wait_ge(s_sub, 4 * (v - 2))
                        nc.scalar.activation(pr[:], pr[:], ACT.Exp, scale=D ** -0.5).then_inc(s_pr, 1)
                if step == 1 and odd and is_batch(b + 1):
                    act.wait_ge(s_xnT_ps, b + 2)
                    wait(act, s_vy_ps, b + 1)
                    nc.scalar.activation(xnT[:], sa[:, :].rearrange("p (k n) -> p k n", k=KC), ACT.Copy
                                         ).then_inc(s_xnT, 1)
                if step == 1 and is_unit(v - 4):
                    act.wait_ge(s_xn3T_ps, v - 3)
                    wait(act, s_lg_ps, v - 4)
                    nc.scalar.activation(xn3T[:], sb_[:, 0:C].rearrange("p (k n) -> p k n", k=KC), ACT.Copy
                                         ).then_inc(s_xn3T, 1)
                if step in (1, 2) and is_unit(v - 3):
                    for i, bk in ((0, xa), (1, xb)):
                        g = 2 * (step - 1) + i
                        act.wait_ge(s_pT_ps, 4 * (v - 3) + g + 1)
                        wait(act, s_pv_ps, v - 3)
                        nc.scalar.activation(pT[:, 4 * g:4 * g + 4, :],
                                             bk[0:NK, :].rearrange("p (h q) -> p h q", h=4), ACT.Copy
                                             ).then_inc(s_pT, 1)
                if step == 3 and odd and is_batch(b + 1):
                    act.wait_ge(s_k_ps, b + 2)
                    nc.scalar.activation(k2[:, nb, :], sa[:, 0:N], ACT.Copy).then_inc(s_k, 1)
                if step == 4:
                    if is_unit(v - 3):
                        act.wait_ge(s_attT_ps, v - 2)
                        wait(act, s_y_ps, v - 3)
                        nc.scalar.activation(attT[:], xb[:, 0:C].rearrange("p (k n) -> p k n", k=KC), ACT.Copy
                                             ).then_inc(s_attT, 1)
                if step == 5:
                    if is_unit(v - 1):
                        act.wait_ge(s_exT_ps, v)
                        wait(act, s_o_ps, v - 1)
                        nc.scalar.activation(exT[:], sa[:, 0:N].rearrange("p (k n) -> p k n", k=2), ACT.Copy
                                             ).then_inc(s_exT, 1)
                    if is_unit(v - 2):
                        act.wait_ge(s_xn2T_ps, v - 1)
                        wait(act, s_qT_ps, v - 2)
                        nc.scalar.activation(xn2T[:], xa[:, 0:C].rearrange("p (k n) -> p k n", k=KC), ACT.Copy
                                             ).then_inc(s_xn2T, 1)
                if step == 6 and is_unit(v - 2):
                    act.wait_ge(s_qT_ps, v - 1)
                    wait(act, s_xs_ps, 4 * (v - 2))
                    for k in range(KC):
                        nc.scalar.activation(qT[:, k, :], xb[:, k * P:(k + 1) * P], ACT.Identity,
                                             bias=xbq_s[:, k:k + 1]).then_inc(s_qT, 1)

            slots(act, slot)
            moe_gelu(act)

        @block.tensor
        def _(pe):
            pe.wait_ge(s_const, 16 * len(consts))
            pe.wait_ge(s_setup, SETUP - 2)
            nc.tensor.matmul(xa[:, 0:C], minus_rho[:], we_s[0:A, 0:C], start=True, stop=True).then_inc(s_vb_ps, 1)
            pe.wait_ge(s_setup, SETUP)

            def scores(v, c, step, first):
                for p in range(first, first + GROUPS):
                    g, s = p % GROUPS, 2 * step + p // GROUPS
                    op = nc.tensor.matmul(score_bank[c % 2][32 * g:32 * g + 32, 0:N], selw[:, s, :],
                                          e[:, c % 2, step, p, :], start=(s == 0), stop=(s == SIDE - 1),
                                          tile_position=(0, 32 * g))
                if step == STEPS - 1 and first:
                    op.then_inc(s_scores, 1)

            def spread(n, par, j, m):
                s, g = 2 * j + m // 2, 2 * (m % 2)
                wait(pe, s_summed, 32 * n + 4 * j + m - 1)
                nc.tensor.matmul(weight_bank[m % 2][:, :], selb[:, s, :], g3[:, par, g:g + 2, :],
                                 start=True, stop=True).then_inc(s_wb, 1)

            def slot(v, b, c):
                odd, last = c % 2, (c + 1) % 2
                for step in range(STEPS):
                    n, par, j = (v - 1, last, step - LAG) if step >= LAG else (v - 2, odd, step + STEPS - LAG)
                    if is_unit(v):
                        pe.wait_ge(s_sqrt, 8 * v + step + 1)
                        if step == 0:
                            wait(pe, s_ex, v - 1)
                    if is_unit(n) and j == 0:
                        pe.wait_ge(s_g3, 192 * (n + 1))
                    for m in range(4):
                        if is_unit(n):
                            spread(n, par, j, m)
                        if is_unit(v) and m % 2 == 0:
                            scores(v, c, step, 2 * m)
                        if m == 1:
                            cross(v, b, c, step)
                        if m == 3:
                            self_attention(v, b, c, step)

            def self_attention(v, b, c, step):
                odd, last, pb = c % 2, (c + 1) % 2, c // 2
                nb = (pb + odd) % 2
                if odd and is_batch(b + 1):
                    if step == 1:
                        pe.wait_ge(s_xn1, 2 * (b + 2))
                        wait(pe, s_exT, v - 1)
                        for r in range(2):
                            for k in range(KC):
                                op = nc.tensor.transpose(sa[:, k * N + r * P:k * N + r * P + P],
                                                         xin[:, r, k * P:(k + 1) * P], ident[:])
                        op.then_inc(s_xnT_ps, 1)
                    if step == 2:
                        pe.wait_ge(s_xnT, b + 2)
                        for k in range(KC):
                            op = nc.tensor.matmul(sa[:, 0:N], wq_s[:, k, :], xnT[:, k, :],
                                                  start=(k == 0), stop=(k == KC - 1))
                        op.then_inc(s_q_ps, 1)
                    if step == 3:
                        pe.wait_ge(s_q, 2 * (b + 2))
                        for k in range(KC):
                            op = nc.tensor.matmul(sa[:, 0:N], wk_s[:, k, :], xnT[:, k, :],
                                                  start=(k == 0), stop=(k == KC - 1))
                        op.then_inc(s_k_ps, 1)
                    if step == 5:
                        if is_unit(v - 1):
                            pe.wait_ge(s_exT, v)
                        else:
                            pe.wait_ge(s_k, b + 2)
                        for r in range(2):
                            for k in range(KC):
                                op = nc.tensor.matmul(sa[:, r * C:(r + 1) * C], xnT[:, k, r * P:(r + 1) * P],
                                                      wy_s[:, k, :], start=(k == 0), stop=(k == KC - 1))
                        op.then_inc(s_vy_ps, 1)
                if step == 0 and is_unit(v - 4):
                    pe.wait_ge(s_xn3, v - 3)
                    wait(pe, s_sub, 4 * (v - 2) if is_unit(v - 3) else 4 * (v - 3))
                    for k in range(KC):
                        op = nc.tensor.transpose(sb_[:, k * P:(k + 1) * P], xn3[:, k * P:(k + 1) * P], ident[:])
                    op.then_inc(s_xn3T_ps, 1)
                if step == 3 and is_unit(v - 2):
                    pe.wait_ge(s_ew2, 2 * (v - 1))
                    pe.wait_ge(s_exT, v - 1)
                    pe.wait_ge(s_vy, b)
                    wait(pe, s_x1, v - 2)
                    wait(pe, s_xn3T, v - 3)
                    vb = (pb + 1) % 2
                    for r in range(2):
                        nc.tensor.matmul(sb_[:, 0:C + 1], exT[:, r, :], vy[:, vb, r, :],
                                         start=(r == 0), stop=False)
                    nc.tensor.matmul(sb_[:, 0:C + 1], ew2[:].rearrange("p g i s -> p (g i s)"), we_s[:],
                                     start=False, stop=True).then_inc(s_o_ps, 1)
                if step == 4:
                    if is_unit(v - 1):
                        pe.wait_ge(s_ex, v)
                        if odd and is_batch(b + 1):
                            pe.wait_ge(s_k, b + 2)
                        if not odd and is_batch(b):
                            pe.wait_ge(s_vy, b + 1)
                        for r in range(2):
                            op = nc.tensor.transpose(sa[:, r * P:(r + 1) * P], ex[:, r * P:(r + 1) * P], ident[:])
                        op.then_inc(s_exT_ps, 1)
                    if not odd and is_batch(b - 1):
                        pe.wait_ge(s_ctx_in, 16 * b)
                        pe.wait_ge(s_x1, v - 1)
                        for k in range(KC):
                            for h in range(2):
                                nc.tensor.matmul(sb_[:, k * NK:(k + 1) * NK], xwk_s[:, h, k * P:(k + 1) * P],
                                                 cT[:, h, :], start=(h == 0), stop=(h == 1))
                        for h in range(2):
                            op = nc.tensor.matmul(sb_[0:NK, C:2 * C], cT[:, h, :], xwv_s[:, h, :],
                                                  start=(h == 0), stop=(h == 1))
                        op.then_inc(s_kv_ps, 1)

            def head_scores(n, g, bk):
                k, h = g // 2, 4 * (g % 2)
                nc.tensor.matmul(bk[:, 0:4 * NK], qT[:, k, :], kbd[:, k, h:h + 4, :], start=True, stop=True
                                 ).then_inc(s_xs_ps, 1)

            def cross(v, b, c, step):
                n, late = v - 2, v - 3
                if step == 7 and is_unit(n):
                    pe.wait_ge(s_qT, 2 * (n + 1))
                    pe.wait_ge(s_kbd, b)
                    wait(pe, s_x2, n)
                    head_scores(n, 0, xa)
                    head_scores(n, 1, xb)
                    if is_unit(v - 4):
                        pe.wait_ge(s_base, v - 3)
                        pe.wait_ge(s_rank, v - 3)
                    wait(pe, s_exT, n + 2 if is_unit(n + 1) else n + 1)
                    if c % 2 == 1 and is_batch(b + 1):
                        pe.wait_ge(s_vy, b + 2)
                    pe.wait_ge(s_x1, n + 1)
                    if c % 2 == 0:
                        pe.wait_ge(s_vx, b)
                    head_scores(n, 2, sa)
                    head_scores(n, 3, sb_)
                if step in (1, 2) and is_unit(late):
                    pe.wait_ge(s_pr, late + 1)
                    for i, bk in ((0, xa), (1, xb)):
                        g = 2 * (step - 1) + i
                        if step == 1:
                            pe.wait_ge(s_sub, 4 * (late + 1))
                        else:
                            pe.wait_ge(s_pT, 4 * late + g - 1)
                        for h in range(4):
                            op = nc.tensor.transpose(bk[0:NK, h * P:(h + 1) * P], pr[:, 4 * g + h, :], ident[:])
                        op.then_inc(s_pT_ps, 1)
                if step == 3 and is_unit(late):
                    pe.wait_ge(s_pT, 4 * (late + 1))
                    pe.wait_ge(s_vx, b if c % 2 else b - 1)
                    for h in range(H):
                        op = nc.tensor.matmul(xa[:, h * (D + 1):(h + 1) * (D + 1)], pT[:, h, :], vx[:, h, :],
                                              start=True, stop=True)
                    op.then_inc(s_pv_ps, 1)
                if step == 3 and is_unit(v - 4):
                    pe.wait_ge(s_xn3T, v - 3)
                    for k in range(KC):
                        op = nc.tensor.matmul(xb[:, 0:E], xn3T[:, k, :], wr_s[:, k, :],
                                              start=(k == 0), stop=(k == KC - 1))
                    op.then_inc(s_lg_ps, 1)
                if step == 6 and is_unit(v - 4):
                    pe.wait_ge(s_oh, v - 3)
                    if is_unit(v - 2):
                        pe.wait_ge(s_x1, v - 1)
                    if c % 2 == 0 and is_batch(b - 1):
                        pe.wait_ge(s_kT, 2 * b)
                        pe.wait_ge(s_vx, b)
                    for i in range(2):
                        op = nc.tensor.matmul(sb_[:, E * i:E * i + E], tri[:, i, :], oh[:], start=True, stop=True)
                    op.then_inc(s_rank_ps, 1)
                if step == 4 and is_unit(late):
                    pe.wait_ge(s_att, late + 1)
                    wait(pe, s_lg, v - 3)
                    for k in range(KC):
                        op = nc.tensor.transpose(xb[:, k * P:(k + 1) * P],
                                                 att[:].rearrange("p h d -> p (h d)")[:, k * P:(k + 1) * P], ident[:])
                    op.then_inc(s_attT_ps, 1)
                if step == 5:
                    if is_unit(n):
                        pe.wait_ge(s_xn2, n + 1)
                        if is_unit(late):
                            pe.wait_ge(s_att, late + 1)
                        for k in range(KC):
                            op = nc.tensor.transpose(xa[:, k * P:(k + 1) * P], xn2[:, k * P:(k + 1) * P], ident[:])
                        op.then_inc(s_xn2T_ps, 1)
                    if is_unit(late):
                        pe.wait_ge(s_attT, late + 1)
                        for k in range(KC):
                            op = nc.tensor.matmul(xb[:, C:2 * C], attT[:, k, :], xwo_s[:, k, :],
                                                  start=(k == 0), stop=(k == KC - 1))
                        op.then_inc(s_y_ps, 1)
                if step == 6 and is_unit(n):
                    pe.wait_ge(s_xn2T, n + 1)
                    if is_unit(late):
                        pe.wait_ge(s_x2, late + 1)
                    for m in range(2):
                        for k in range(KC):
                            op = nc.tensor.matmul(xb[:, m * P:(m + 1) * P], xwq_s[:, k, m * P:(m + 1) * P],
                                                  xn2T[:, k, :], start=(k == 0), stop=(k == KC - 1))
                    op.then_inc(s_qT_ps, 1)

            slots(pe, slot)
            moe_matmuls(pe)

        @block.vector
        def _(dve):
            nc.vector.memset(eps_rho[:], EPS_RHO).then_inc(s_setup, 1)
            nc.vector.memset(eps_ln[:], EPS_LN).then_inc(s_setup, 1)
            nc.vector.memset(minus_rho[:], -(EPS_RHO ** 0.5)).then_inc(s_setup, 1)
            nc.vector.memset(vy[:, :, :, C:C + 1], 1.0).then_inc(s_setup, 1)
            nc.vector.memset(vx[:, :, D:D + 1], 1.0).then_inc(s_setup, 1)
            nc.vector.memset(we_s[:, C:C + 1], 0.0).then_inc(s_setup, 1)
            nc.vector.memset(ew2[:], 0.0).then_inc(s_setup, 1)
            dve.wait_ge(s_const, 16 * len(consts))
            nc.vector.tensor_scalar(selw[:].rearrange("p s m -> p (s m)"), stage[:, 0:512], phi[:], None, ALU.mult
                                    ).then_inc(s_setup, 1)
            nc.vector.tensor_copy(selb[:].rearrange("p s m -> p (s m)"), stage[0:96, 512:2560]).then_inc(s_setup, 1)
            nc.vector.tensor_copy(base[:], base0).then_inc(s_setup, 1)
            dve.wait_ge(s_vb_ps, 1)
            nc.vector.tensor_tensor(vbias[:], xa[:, 0:C], stage[:, 2560:2816], ALU.add).then_inc(s_setup, 1)
            dve.wait_ge(s_setup, SETUP - 1)
            nc.vector.tensor_tensor(vbias[:], vbias[:], stage[:, 2816:3072], ALU.add).then_inc(s_setup, 1)
            dve.wait_ge(s_setup, SETUP)

            def ln1_stats(b):
                dve.wait_ge(s_x_in, 16 * (b + 1))
                wait(dve, s_mv1, 2 * b)
                wait(dve, s_xn1, 2 * b)
                for r in range(2):
                    nc.vector.bn_stats(st1[:, r, :], xin[:, r, :]).then_inc(s_st1, 1)
                dve.wait_ge(s_st1, 2 * (b + 1))
                take_waits(dve)
                for r in range(2):
                    nc.vector.bn_aggr(mv1[:, r, :], st1[:, r, :]).then_inc(s_mv1, 1)

            def weigh(n, par, j, p):
                s, g = 2 * j + p // 4, p % 4
                if p % 2 == 0:
                    dve.wait_ge(s_wb, 32 * n + 4 * j + p // 2 + 1)
                ep = pair_ap(par, j, p)
                op = nc.vector.tensor_tensor_reduce(
                    out=ep, in0=ep, in1=weight_bank[p // 2 % 2][:, (p % 2) * N:(p % 2) * N + N], scale=1.0,
                    scalar=0.0, op0=ALU.mult, op1=ALU.add, accum_out=ew[:, par, g, s:s + 1])
                if p % 2 == 1:
                    op.then_inc(s_summed, 1)

            def slot(v, b, c):
                odd, last = c % 2, (c + 1) % 2
                for step in range(STEPS):
                    n, par, j = (v - 1, last, step - LAG) if step >= LAG else (v - 2, odd, step + STEPS - LAG)
                    vv, bb, cc, jj = ahead(v, b, c, step)
                    if is_unit(vv):
                        wait_relu(dve, vv, bb, jj)
                    if is_unit(n) and j == 0:
                        wait(dve, s_ew2, 2 * (n - 1))
                    for p in range(CHUNK):
                        if is_unit(n):
                            weigh(n, par, j, p)
                        if is_unit(vv) and p in ON_DVE:
                            op = nc.vector.tensor_scalar(
                                pair_ap(cc % 2, jj, p), k2[:, cc // 2, :], query(cc // 2, cc % 2, jj, p), 0.0,
                                ALU.add, ALU.max)
                            if p == ON_DVE[-1]:
                                op.then_inc(s_relu_dve, 1)
                        if step in (0, 1, 2):
                            softmax(v, b, c, step, p)
                        if step in (3, 4, 5):
                            residual(v, b, c, step, p)
                        cross(v, b, c, step, p)
                        routing(v, b, c, step, p)
                        if step == 7 and not odd and p == 1 and is_batch(b + 1):
                            ln1_stats(b + 1)

            def softmax(v, b, c, step, p):
                odd, last, pb = c % 2, (c + 1) % 2, c // 2
                nb = (pb + 1) % 2
                n = v - 1
                if is_unit(n):
                    if step == 0 and p == 0:
                        dve.wait_ge(s_scores, v)
                        wait(dve, s_ex, n)
                        nc.vector.tensor_reduce(nmax[:], score_bank[last][:, 0:N], AX.X, ALU.max, negate=True
                                                ).then_inc(s_nmax, 1)
                    if step == 0 and p == 6:
                        dve.wait_ge(s_ex, v)
                        wait(dve, s_g3, 192 * n)
                        nc.vector.tensor_copy(parts[:, 0, :], ex[:]).then_inc(s_hi, 1)
                    if step == 0 and p == 7:
                        dve.wait_ge(s_hi, v)
                        nc.vector.tensor_tensor(rem[:], ex[:], parts[:, 0, :], ALU.subtract).then_inc(s_r1, 1)
                    if step == 1 and p == 0:
                        dve.wait_ge(s_r1, v)
                        nc.vector.tensor_copy(parts[:, 1, :], rem[:]).then_inc(s_mid, 1)
                    if step == 1 and p == 1:
                        dve.wait_ge(s_mid, v)
                        nc.vector.tensor_tensor(parts[:, 2, :], rem[:], parts[:, 1, :], ALU.subtract
                                                ).then_inc(s_split, 1)
                if odd and is_batch(b + 1):
                    if step == 0 and p == 2:
                        dve.wait_ge(s_sd1, b + 2)
                        nc.vector.reciprocal(rs1[:], sd1[:]).then_inc(s_rs1, 1)
                    if step == 0 and p == 3:
                        dve.wait_ge(s_rs1, b + 2)
                        for r in range(2):
                            nc.vector.tensor_scalar(xin[:, r, :], xin[:, r, :], mv1[:, r, 0:1], rs1[:, r:r + 1],
                                                    ALU.subtract, ALU.mult).then_inc(s_xn1, 1)
                    if step == 2 and p == 7:
                        dve.wait_ge(s_q_ps, b + 2)
                        wait(dve, s_relu_act, 8 * (v - 1))
                        wait(dve, s_relu_pool, 8 * (v - 1))
                        wait(dve, s_relu_dve, 8 * (v - 1))
                        for i in range(2):
                            half = slice(A * i, A * i + A)
                            nc.vector.tensor_copy(
                                q2[half, nb, :, :, :].rearrange("p u g s -> p (u g) s"),
                                sa[half, 0:N].rearrange("p (w i s) -> p w i s", i=2, s=SIDE)[:, :, i, :]
                            ).then_inc(s_q, 1)
                if step == 2 and p == 2 and is_unit(v - 2):
                    dve.wait_ge(s_summed, 32 * (v - 1))
                    wait(dve, s_o_ps, v - 2)
                    for i in range(2):
                        half = slice(A * i, A * i + A)
                        nc.vector.tensor_copy(ew2[half, :, i, :], ew[half, odd, :, :]).then_inc(s_ew2, 1)

            def residual(v, b, c, step, p):
                odd, pb = c % 2, c // 2
                nb = (pb + 1) % 2
                n = v - 2
                if is_unit(n):
                    if step == 4 and p == 0:
                        dve.wait_ge(s_o_ps, n + 1)
                        wait(dve, s_rden, n)
                        nc.vector.tensor_scalar(den[:], sb_[:, C:C + 1], EPS_DEN, None, ALU.add).then_inc(s_den, 1)
                    if step == 4 and p == 1:
                        dve.wait_ge(s_den, n + 1)
                        wait(dve, s_x1, n)
                        nc.vector.reciprocal(rden[:], den[:]).then_inc(s_rden, 1)
                    if step == 4 and p == 2:
                        dve.wait_ge(s_rden, n + 1)
                        dve.wait_ge(s_res_in, 16 * (n + 1))
                        wait(dve, s_x1b, n)
                        wait(dve, s_xn2, n)
                        nc.vector.scalar_tensor_tensor(x1[:], sb_[:, 0:C], rden[:], xres[:, odd, :],
                                                       ALU.mult, ALU.add).then_inc(s_x1, 1)
                    if step == 4 and p == 3:
                        dve.wait_ge(s_x1, n + 1)
                        wait(dve, s_mv2, n)
                        nc.vector.bn_stats(st2[:], x1[:]).then_inc(s_st2, 1)
                    if step == 4 and p == 4:
                        dve.wait_ge(s_st2, n + 1)
                        take_waits(dve)
                        nc.vector.bn_aggr(mv2[:], st2[:]).then_inc(s_mv2, 1)
                    if step == 5 and p == 0:
                        dve.wait_ge(s_sd2, n + 1)
                        nc.vector.reciprocal(rs2[:], sd2[:]).then_inc(s_rs2, 1)
                    if step == 5 and p == 1:
                        dve.wait_ge(s_rs2, n + 1)
                        wait(dve, s_xn2T_ps, n)
                        nc.vector.tensor_scalar(xn2[:], x1[:], mv2[:, 0:1], rs2[:], ALU.subtract, ALU.mult
                                                ).then_inc(s_xn2, 1)
                if step == 4 and p == 7 and not odd and is_batch(b - 1):
                    dve.wait_ge(s_kv_ps, b)
                    wait(dve, s_kbd, b - 1)
                    wait(dve, s_pv_ps, v - 2)
                    for k in range(KC):
                        nc.vector.tensor_scalar(kT[:, k, :], sb_[:, k * NK:(k + 1) * NK], xbk_s[:, k:k + 1], None,
                                                ALU.add).then_inc(s_kT, 1)
                    nc.vector.tensor_tensor(vx[:, :, 0:D], sb_[0:NK, C:2 * C].rearrange("p (h d) -> p h d", h=H),
                                            xbv_s[:].rearrange("p (h d) -> p h d", h=H), ALU.add).then_inc(s_vx, 1)

            def routing(v, b, c, step, p):
                odd = c % 2
                n, z, w = v - 3, v - 4, v - 5
                if is_unit(n):
                    row = pay[:, 1 - odd, :]
                    if step == 6 and p == 3:
                        dve.wait_ge(s_x2, n + 1)
                        wait(dve, s_mv3, n)
                        nc.vector.bn_stats(st3[:], row[:, 0:C]).then_inc(s_st3, 1)
                    if step == 6 and p == 5:
                        dve.wait_ge(s_st3, n + 1)
                        take_waits(dve)
                        nc.vector.bn_aggr(row[:, AT_MEAN:AT_SCALE + 1], st3[:]).then_inc(s_mv3, 1)
                    if step == 7 and p == 1:
                        dve.wait_ge(s_sd3, n + 1)
                        nc.vector.reciprocal(row[:, AT_SCALE:AT_SCALE + 1], sd3[:]).then_inc(s_rs3, 1)
                    if step == 7 and p == 4:
                        dve.wait_ge(s_rs3, n + 1)
                        wait(dve, s_xn3T_ps, n)
                        nc.vector.tensor_scalar(xn3[:], row[:, 0:C], row[:, AT_MEAN:AT_MEAN + 1],
                                                row[:, AT_SCALE:AT_SCALE + 1], ALU.subtract, ALU.mult
                                                ).then_inc(s_xn3, 1)
                if is_unit(z):
                    if step == 3 and p == 7:
                        dve.wait_ge(s_lg_ps, z + 1)
                        wait(dve, s_els, z)
                        nc.vector.tensor_tensor(lg[:], xb[:, 0:E], br_s[:], ALU.add).then_inc(s_lg, 1)
                    if step == 4 and p == 5:
                        dve.wait_ge(s_lg, z + 1)
                        wait(dve, s_lsub, z)
                        nc.vector.tensor_reduce(nlmax[:], lg[:], AX.X, ALU.max, negate=True).then_inc(s_lmax, 1)
                    if step == 4 and p == 6:
                        dve.wait_ge(s_lmax, z + 1)
                        nc.vector.tensor_scalar(lg[:], lg[:], nlmax[:], None, ALU.add).then_inc(s_lsub, 1)
                    if step == 5 and p == 2:
                        dve.wait_ge(s_lsub, z + 1)
                        wait(dve, s_oh, z)
                        nc.vector.scalar_tensor_tensor(key[:], lg[:], 0.0, tie, ALU.is_ge, ALU.mult
                                                       ).then_inc(s_key, 1)
                    if step == 5 and p == 3:
                        dve.wait_ge(s_key, z + 1)
                        nc.vector.tensor_reduce(kmax[:], key[:], AX.X, ALU.max).then_inc(s_kmax, 1)
                    if step == 5 and p == 4:
                        dve.wait_ge(s_kmax, z + 1)
                        wait(dve, s_pos, z)
                        wait(dve, s_rank_ps, z)
                        nc.vector.tensor_scalar(oh[:], key[:], kmax[:], None, ALU.is_equal).then_inc(s_oh, 1)
                    if step == 6 and p == 6:
                        dve.wait_ge(s_rank_ps, z + 1)
                        wait(dve, s_base, z)
                        nc.vector.tensor_tensor(rank[:], sb_[:, 0:E], base[:], ALU.add).then_inc(s_rank, 1)
                    if step == 6 and p == 7:
                        dve.wait_ge(s_rank, z + 1)
                        nc.vector.tensor_tensor(base[:], sb_[:, E:2 * E], base[:], ALU.add).then_inc(s_base, 1)
                    if step == 7 and p == 7:
                        wait(dve, s_posi, z)
                        nc.vector.tensor_tensor_reduce(out=rank[:], in0=oh[:], in1=rank[:], scale=1.0, scalar=0.0,
                                                       op0=ALU.mult, op1=ALU.add, accum_out=pos[:]
                                                       ).then_inc(s_pos, 1)
                if is_unit(w):
                    if step == 1 and p == 3:
                        dve.wait_ge(s_els, w + 1)
                        nc.vector.reciprocal(pay[:, 1 - odd, AT_WEIGHT:AT_WEIGHT + 1], sume[:]).then_inc(s_wt, 1)
                    if step == 1 and p == 4:
                        dve.wait_ge(s_pos, w + 1)
                        wait(dve, s_scat, 16 * w)
                        nc.vector.tensor_copy(posi[:], pos[:]).then_inc(s_posi, 1)

            def cross(v, b, c, step, p):
                odd, pb = c % 2, c // 2
                nb = (pb + 1) % 2
                n, late = v - 2, v - 3
                if step == 6 and p == 1 and odd and is_batch(b + 1):
                    dve.wait_ge(s_vy_ps, b + 2)
                    wait(dve, s_o_ps, v - 1)
                    nc.vector.tensor_tensor(vy[:, nb, :, 0:C], sa[:, :].rearrange("p (r c) -> p r c", r=2),
                                            vbias[:].unsqueeze(1).to_broadcast([P, 2, C]), ALU.add).then_inc(s_vy, 1)
                if is_unit(late):
                    if step == 3 and p == 5:
                        dve.wait_ge(s_pv_ps, late + 1)
                        wait(dve, s_att, late)
                        pv = xa[:, 0:H * (D + 1)].rearrange("p (h d) -> p h d", h=H)
                        nc.vector.reciprocal(hden[:], pv[:, :, D]).then_inc(s_hden, 1)
                    if step == 3 and p == 6:
                        dve.wait_ge(s_hden, late + 1)
                        wait(dve, s_attT_ps, late)
                        pv = xa[:, 0:H * (D + 1)].rearrange("p (h d) -> p h d", h=H)
                        nc.vector.tensor_tensor(att[:], pv[:, :, 0:D], hden[:].unsqueeze(2).to_broadcast([P, H, D]),
                                                ALU.mult).then_inc(s_att, 1)
                    if step == 5 and p == 6:
                        dve.wait_ge(s_y_ps, late + 1)
                        dve.wait_ge(s_x1b, late + 1)
                        wait(dve, s_scat, 16 * (late - 1))
                        nc.vector.tensor_tensor(pay[:, 1 - odd, 0:C], xb[:, C:2 * C], x1b[:], ALU.add
                                                ).then_inc(s_x2, 1)
                if step == 7 and is_unit(n) and p in (2, 3, 5, 6):
                    g = (2, 3, 5, 6).index(p)
                    bk = (xa, xb, sa, sb_)[g][:, 0:4 * NK].rearrange("p (h k) -> p h k", h=4)
                    dve.wait_ge(s_xs_ps, 4 * n + g + 1)
                    wait(dve, s_sub, 4 * n)
                    wait(dve, s_pT_ps, 4 * n)
                    nc.vector.tensor_reduce(hmax[:, 4 * g:4 * g + 4], bk, AX.X, ALU.max).then_inc(s_hmax, 1)
                    dve.wait_ge(s_hmax, 4 * n + g + 1)
                    nc.vector.tensor_tensor(pr[:, 4 * g:4 * g + 4, :], bk,
                                            hmax[:, 4 * g:4 * g + 4].unsqueeze(2).to_broadcast([P, 4, NK]),
                                            ALU.subtract).then_inc(s_sub, 1)

            ln1_stats(0)
            slots(dve, slot)
            moe_vector(dve)


def kernel(x, ctx_768, L0_attn_Wq, L0_attn_Wk, L0_attn_Wphi, L0_attn_Wy_w, L0_attn_Wy_b, L0_attn_We_w, L0_attn_We_b,
           L0_xattn_Wq, L0_xattn_bq, L0_xattn_Wk, L0_xattn_bk, L0_xattn_Wv, L0_xattn_bv, L0_xattn_Wo, L0_xattn_bo,
           L0_ffn_Wr, L0_ffn_br, L0_ffn_W1, L0_ffn_b1, L0_ffn_W2, L0_ffn_b2):
    import numpy as np
    import concourse.bacc as bacc
    from concourse import mybir as mb
    from concourse.bass_utils import run_bass_kernel_spmd as run

    def chunks(w, p):
        w = np.asarray(w)
        return w.reshape(w.shape[0] // p, p, -1).transpose(1, 0, 2)

    def rows(w, n):
        return np.tile(np.asarray(w).reshape(1, -1), (n, 1))

    m, s = np.arange(32), np.arange(16)
    half = np.arange(P) // A
    selw = (m[None, None, :] == 16 * half[:, None, None] + s[None, :, None]).astype(np.float32)
    k = np.arange(96) % 32
    selb = (k[:, None, None] == 16 * half[None, None, :] + s[None, :, None]).astype(np.float32)
    headmask = (np.arange(P)[:, None] // 16 == np.arange(8)[None, :]).astype(np.float32)
    route = np.concatenate([rows(np.arange(E, 0, -1), P), rows(REGION * np.arange(E), P),
                            rows(P * np.arange(UNITS), P), rows(np.arange(TILES), P),
                            np.arange(P)[:, None]], 1).astype(np.float32)
    arrays = {
        "x": np.asarray(x),
        "ctxT": np.asarray(ctx_768).transpose(2, 0, 1).reshape(2, CC, B, NK).transpose(1, 2, 0, 3),
        "wq": chunks(np.asarray(L0_attn_Wq).T, P), "wk": chunks(np.asarray(L0_attn_Wk).T, P),
        "wphi": np.asarray(L0_attn_Wphi).reshape(A, 1),
        "wy": chunks(np.asarray(L0_attn_Wy_w).T, P), "wy_b": rows(L0_attn_Wy_b, P),
        "we": np.asarray(L0_attn_We_w).T, "we_b": rows(L0_attn_We_b, P),
        "xwq": chunks(L0_xattn_Wq, P), "xbq": np.asarray(L0_xattn_bq).reshape(KC, P).T,
        "xwk": chunks(L0_xattn_Wk, CC), "xbk": np.asarray(L0_xattn_bk).reshape(KC, P).T,
        "xwv": chunks(L0_xattn_Wv, CC), "xbv": rows(L0_xattn_bv, NK),
        "xwo": chunks(L0_xattn_Wo, P), "xbo": rows(L0_xattn_bo, P),
        "wr": chunks(L0_ffn_Wr, P), "br": rows(L0_ffn_br, P),
        "w1": np.asarray(L0_ffn_W1).reshape(E, KC, P, F).transpose(2, 0, 1, 3),
        "w2": np.asarray(L0_ffn_W2).reshape(E, F // P, P, C).transpose(2, 0, 1, 3),
        "b12": np.concatenate([np.asarray(L0_ffn_b1).ravel(), np.asarray(L0_ffn_b2).ravel()]).reshape(P, -1),
        "ident": np.eye(P, dtype=np.float32), "tri": np.stack([np.triu(np.ones((P, P), np.float32), 1),
                                                               np.ones((P, P), np.float32)], 1), "selw": selw.reshape(P, 512), "selb": selb.reshape(96, 2048),
        "headmask": headmask, "route": route,
    }
    arrays = {f"in_{k}": np.ascontiguousarray(v) for k, v in arrays.items()}
    nc = bacc.Bacc("TRN2", target_bir_lowering=False, num_devices=1)
    args = [nc.dram_tensor(k, v.shape, mb.dt.from_np(v.dtype), kind="ExternalInput").ap() for k, v in arrays.items()]
    args.append(nc.dram_tensor("out", (B, N, C), mb.dt.float32, kind="ExternalOutput").ap())
    decoder_args = dict(zip(["x", "ctxT", "wq", "wk", "wphi", "wy", "wy_b", "we", "we_b", "xwq", "xbq", "xwk", "xbk",
                             "xwv", "xbv", "xwo", "xbo", "wr", "br", "w1", "w2", "b12", "ident_h", "tri_h", "selw_h",
                             "selb_h", "headmask_h", "route_h", "out"], args))
    decoder(nc, **decoder_args)
    return run(nc, [arrays], core_ids=[0]).results[0]["out"]
```

```python
import concourse.bass as bass
from concourse import mybir
from contextlib import ExitStack

F32 = mybir.dt.float32
BF16 = mybir.dt.bfloat16
ALU = mybir.AluOpType
ACT = mybir.ActivationFunctionType
AX = mybir.AxisListType
I32 = mybir.dt.int32

B, N, C, A = 32, 256, 256, 64
CD, NK, H, D = 192, 77, 16, 16
E, F = 8, 512
P = 128
UNITS = B * N // P
PAIRS = P // 2
CHUNK = 8
STEPS = PAIRS // CHUNK
GROUPS = 4
SIDE = PAIRS // GROUPS
KC = C // P
CC = CD // 2
LAG = 3
RELU_AHEAD, SQRT_AHEAD = 3, 1
HEADS_AT = (1, 3, 4, 6)
REGION = B * N + P
TILES = B * N // P + E
ROW = C + 4
AT_ID, AT_WEIGHT, AT_MEAN, AT_SCALE = range(C, C + 4)
ROUTE = 16 + B * N // P + TILES + 1
NO_ROW = 2.0 * B * N
EPS_RHO, EPS_DEN, EPS_LN = 1e-8, 1e-9, 1e-5
POOL_SHARE, ACT_SHARE = (2, 3, 3, 3, 3, 3, 3, 3), (2, 2, 3, 4, 4, 4, 4, 4)
SPREAD = (0, 4, 2, 6, 1, 5, 3, 7)


def relu_pairs(v, step):
    pool_share, act_share = POOL_SHARE[step], ACT_SHARE[step]
    if isinstance(v, int) and v <= 0:
        pool_share, act_share = 1, 1
    dve = CHUNK - pool_share - act_share
    pool = dve + pool_share
    return sorted(SPREAD[:dve]), sorted(SPREAD[dve:pool]), sorted(SPREAD[pool:])


def wait(eng, sem, n):
    if isinstance(n, int) and n <= 0:
        return
    eng.wait_ge(sem, n)


def is_unit(n):
    return not isinstance(n, int) or 0 <= n < UNITS


def is_tile(t):
    return not isinstance(t, int) or 0 <= t < TILES


def is_batch(n):
    return not isinstance(n, int) or 0 <= n < B


def decoder(nc, x, ctxT, wq, wk, wphi, wy, wy_b, we, we_b, xwq, xbq, xwk, xbk, xwv, xbv, xwo, xbo,
            wr, br, w1, w2, b12, ident_h, tri_h, selw_h, selb_h, headmask_h, route_h, out):
    rows = x.rearrange("b (u p) c -> p (b u) c", p=P)
    out_rows = out.rearrange("b n c -> (b n) c")
    regions = nc.dram_tensor("regions", (E * REGION + P, ROW), F32, kind="Internal").ap()

    with ExitStack() as ctx:
        def sb(name, shape, dt=F32):
            return ctx.enter_context(nc.sbuf_tensor(name, shape, dt))

        def sem(name):
            return ctx.enter_context(nc.semaphore(name))

        bank = [ctx.enter_context(nc.psum_tensor(f"bank{i}", [P, 512], F32)) for i in range(8)]
        score_bank = [bank[0][:, N * i:N * i + N] for i in range(2)]
        weight_bank = bank[1:5]
        work0, work1, work2 = bank[5], bank[6], bank[7]
        out_ps, rank_ps, logit_ps = work1[:, E:E + C + 1], work0[:, 0:2 * E], work1[:, 0:E]
        exT_ps, xn2T_ps, qT_ps, y_ps = work2[:, N:2 * N], work1[:, 0:C], work1[:, C:2 * C], work0[:, 0:C]
        k_ctx_ps, v_ctx_ps = work2[:, C:C + KC * NK], work2[0:NK, 0:C]

        e = sb("e", [P, 2, STEPS, CHUNK, N])
        ident = sb("ident", [P, P])
        eps_rho = sb("eps_rho", [P, 1])
        eps_ln = sb("eps_ln", [P, 1])
        phi = sb("phi", [P, 1])
        selw = sb("selw", [P, SIDE, 32])
        selb = sb("selb", [3 * 32, SIDE, P], BF16)
        wq_s = sb("wq_s", [P, KC, P])
        wk_s = sb("wk_s", [P, KC, P])
        wy_s = sb("wy_s", [P, KC, C])
        we_s = sb("we_s", [P, C + 1])
        vbias = sb("vbias", [P, C])
        minus_rho = sb("minus_rho", [A, P])
        xin = sb("xin", [P, 2, C])
        xnT = sb("xnT", [P, KC, N])
        st1 = sb("st1", [P, 2, 6])
        mv1 = sb("mv1", [P, 2, 2])
        sd1 = sb("sd1", [P, 2])
        rs1 = sb("rs1", [P, 2])
        k2 = sb("k2", [P, 2, N])
        q2 = sb("q2", [P, 2, 2, GROUPS, SIDE])
        vy = sb("vy", [P, 2, 2, C + 1])
        nmax = sb("nmax", [P, 1])
        ex = sb("ex", [P, N])
        rem = sb("rem", [P, N])
        parts = sb("parts", [P, 3, N], BF16)
        g3 = sb("g3", [3 * 32, 2, GROUPS, N], BF16)
        exT = sb("exT", [P, 2, P])
        ew = sb("ew", [P, 2, GROUPS, SIDE])
        ew2 = sb("ew2", [P, GROUPS, 2, SIDE])
        xres = sb("xres", [P, 2, C])
        den = sb("den", [P, 1])
        rden = sb("rden", [P, 1])
        x1 = sb("x1", [P, C])
        xwq_s = sb("xwq_s", [P, KC, C])
        xwk_s = sb("xwk_s", [CC, 2, C])
        xwv_s = sb("xwv_s", [CC, 2, C])
        xwo_s = sb("xwo_s", [P, KC, C])
        xbq_s = sb("xbq_s", [P, KC])
        xbk_s = sb("xbk_s", [P, KC])
        xbv_s = sb("xbv_s", [NK, C])
        xbo_s = sb("xbo_s", [P, C])
        headmask = sb("headmask", [P, H // 2])
        cT = sb("cT", [CC, 2, NK])
        kT = sb("kT", [P, KC, NK])
        kbd = sb("kbd", [P, KC, H // 2, NK])
        vx = sb("vx", [NK, H // 2, 2, 2 * D])
        vones = sb("vones", [NK, 2, 2 * D])
        st2 = sb("st2", [P, 6])
        mv2 = sb("mv2", [P, 2])
        sd2 = sb("sd2", [P, 1])
        rs2 = sb("rs2", [P, 1])
        xn2 = sb("xn2", [P, C])
        xn2T = sb("xn2T", [P, KC, P])
        qT = sb("qT", [P, KC, P])
        hmax = sb("hmax", [P, H])
        pr = sb("pr", [P, H, NK])
        pT = sb("pT", [NK, H, P])
        rhden = rem
        attT = sb("attT", [P, KC, P])
        x1b = sb("x1b", [P, C])
        pay = sb("pay", [P, 2, ROW])
        st3 = sb("st3", [P, 6])
        sd3 = sb("sd3", [P, 1])
        xn3 = xn2
        xn3T = sb("xn3T", [P, KC, P])
        wr_s = sb("wr_s", [P, KC, E])
        br_s = sb("br_s", [P, E])
        tri = sb("tri", [P, 2, P])
        route = sb("route", [P, ROUTE])
        tie, base0 = route[:, 0:E], route[:, E:2 * E]
        full, tile_no = route[:, 16:16 + UNITS], route[:, 16 + UNITS:ROUTE - 1]
        row_id = route[:, ROUTE - 1:ROUTE]
        lg = sb("lg", [P, E])
        nlmax = sb("nlmax", [P, 1])
        key = sb("key", [P, E])
        kmax = sb("kmax", [P, 1])
        oh = sb("oh", [P, E])
        base = sb("base", [P, E])
        rank = sb("rank", [P, E])
        pos = sb("pos", [P, 1])
        posi = sb("posi", [P, 1], I32)
        els = sb("els", [P, E])
        sume = sb("sume", [P, 1])

        s_const = sem("consts_loaded")
        s_setup = sem("setup_vector")
        s_vb_ps = sem("vbias_psum")
        s_x_in = sem("x_loaded")
        s_ctx_in = sem("context_loaded")
        s_res_in = sem("residual_loaded")
        s_st1 = sem("ln1_stats")
        s_mv1 = sem("ln1_variance")
        s_sd1 = sem("ln1_deviation")
        s_rs1 = sem("ln1_scale")
        s_xn1 = sem("ln1_rows")
        s_xnT_ps = sem("xnT_in_psum")
        s_xnT = sem("xnT_ready")
        s_q_ps = sem("q_in_psum")
        s_q = sem("q_ready")
        s_k_ps = sem("k_in_psum")
        s_k = sem("k_ready")
        s_vy_ps = sem("vy_in_psum")
        s_vy = sem("vy_ready")
        s_relu_dve = sem("relu_vector")
        s_relu_act = sem("relu_scalar")
        s_relu_pool = sem("relu_pool")
        s_sqrt = sem("sqrt_done")
        s_scores = sem("scores_ready")
        s_nmax = sem("negmax_ready")
        s_ex = sem("exp_ready")
        s_hi = sem("hi_ready")
        s_r1 = sem("rest1_ready")
        s_mid = sem("mid_ready")
        s_split = sem("split_ready")
        s_g3 = sem("g3_loaded")
        s_wb = sem("weights_in_psum")
        s_summed = sem("pairs_summed")
        s_exT_ps = sem("exT_in_psum")
        s_exT = sem("exT_ready")
        s_ew2 = sem("ew2_ready")
        s_o_ps = sem("o_in_psum")
        s_den = sem("den_ready")
        s_rden = sem("rden_ready")
        s_x1 = sem("x1_ready")
        s_st2 = sem("ln2_stats")
        s_mv2 = sem("ln2_variance")
        s_sd2 = sem("ln2_deviation")
        s_rs2 = sem("ln2_scale")
        s_xn2 = sem("ln2_rows")
        s_xn2T_ps = sem("xn2T_in_psum")
        s_xn2T = sem("xn2T_ready")
        s_qT_ps = sem("qT_in_psum")
        s_qT = sem("qT_ready")
        s_kv_ps = sem("kv_in_psum")
        s_kT = sem("kT_ready")
        s_vx = sem("vx_ready")
        s_kbd = sem("kbd_ready")
        s_xs_ps = sem("xscores_in_psum")
        s_hmax = sem("head_max_ready")
        s_sub = sem("xscores_shifted")
        s_pr = sem("probs_ready")
        s_pT_ps = sem("pT_in_psum")
        s_pT = sem("pT_ready")
        s_pv_ps = sem("pv_in_psum")
        s_hden = sem("head_scale_ready")
        s_attT = sem("attT_ready")
        s_x1b = sem("x1_with_bias")
        s_y_ps = sem("xattn_out_in_psum")
        s_x2 = sem("x2_ready")
        s_st3 = sem("ln3_stats")
        s_mv3 = sem("ln3_variance")
        s_sd3 = sem("ln3_deviation")
        s_rs3 = sem("ln3_scale")
        s_xn3 = sem("ln3_rows")
        s_xn3T_ps = sem("xn3T_in_psum")
        s_xn3T = sem("xn3T_ready")
        s_lg_ps = sem("logits_in_psum")
        s_lg = sem("logits_ready")
        s_lmax = sem("logit_max_ready")
        s_lsub = sem("logits_shifted")
        s_key = sem("key_ready")
        s_kmax = sem("key_max_ready")
        s_oh = sem("onehot_ready")
        s_rank_ps = sem("rank_in_psum")
        s_rank = sem("rank_ready")
        s_base = sem("base_moved")
        s_pos = sem("position_ready")
        s_posi = sem("position_integer")
        s_els = sem("logit_exp_ready")
        s_wt = sem("weight_ready")
        s_id = sem("row_number_written")
        s_idn = sem("row_number_moved")
        s_scat = sem("rows_scattered")

        stage = e[:].rearrange("p u j q n -> p (u j q n)")
        consts = [
            (ident[:], ident_h), (phi[0:A, :], wphi), (phi[A:P, :], wphi), (stage[:, 0:512], selw_h),
            (stage[0:96, 512:2560], selb_h), (wq_s[:, :, 0:A], wq), (wq_s[:, :, A:P], wq), (wk_s[:, :, 0:A], wk),
            (wk_s[:, :, A:P], wk), (wy_s[:], wy), (we_s[0:A, 0:C], we), (we_s[A:P, 0:C], we),
            (stage[:, 2560:2816], wy_b), (stage[:, 2816:3072], we_b), (xwq_s[:], xwq), (xwk_s[:], xwk), (xwv_s[:], xwv),
            (xwo_s[:], xwo), (xbq_s[:], xbq), (xbk_s[:], xbk), (xbv_s[:], xbv), (xbo_s[:], xbo),
            (headmask[:], headmask_h), (wr_s[:], wr), (br_s[:], br), (tri[:], tri_h), (route[:], route_h),
        ]
        SETUP = 14
        block = ctx.enter_context(nc.Block())

        s_taken = sem("waits_taken")

        def own_half(t):
            return t.rearrange("p g i (x d) -> p g (i x) d", d=D)[:, :, 0::3, :]

        def take_waits(eng):
            eng.sem_inc(s_taken, 1)

        def slots(eng, slot):
            for v in range(-1, 8):
                slot(v, v // 2, v % 4)
            with eng.Fori(2, UNITS // 4 - 1) as i:
                for c in range(4):
                    slot(4 * i + c, 2 * i + c // 2, c)
            for v in range(UNITS - 4, UNITS + 5):
                slot(v, v // 2, v % 4)

        flat = e[:].rearrange("p u j q n -> p (u j q n)")
        HALF = STEPS * CHUNK * N
        taken = [HALF]

        def room(cols, dt=F32):
            words = cols if dt != BF16 else cols // 2
            at, taken[0] = taken[0], taken[0] + words
            v = flat[:, at:at + words]
            return v if dt == F32 else v.bitcast(dt)

        FC = F // P
        w1_s = flat[:, 0:E * KC * F].rearrange("p (e k f) -> p e k f", e=E, k=KC)
        w2_s = flat[:, E * KC * F:E * (KC * F + FC * C)].rearrange("p (e k c) -> p e k c", e=E, k=FC)
        BIAS = E * (F + C)
        tin = room(4 * ROW).rearrange("p (b r) -> p b r", b=4)
        xnb = room(2 * C).rearrange("p (b c) -> p b c", b=2)
        xnbT = room(2 * C).rearrange("p (b k n) -> p b k n", b=2, k=KC)
        hid = room(2 * F).rearrange("p (b f) -> p b f", b=2)
        hidT = room(2 * F).rearrange("p (b k n) -> p b k n", b=2, k=FC)
        yout = room(2 * C).rearrange("p (b c) -> p b c", b=2)
        rowi = room(2, I32)
        brows = room(BIAS, BF16)[0:3, :]
        bstage = room(BIAS // P)
        brem = room(BIAS // P)
        bsplit = room(3 * BIAS // P + BIAS // P % 2, BF16)[:, 0:3 * BIAS // P].rearrange("p (t n) -> p t n", t=3)
        ones3 = room(P, BF16)[0:3, :]
        fill = room(ROW)
        cnt, ntile, tend, tword = room(E), room(E), room(E), room(E)
        above = room(E * UNITS).rearrange("p (e k) -> p e k", e=E)
        past = room(TILES * E).rearrange("p (t e) -> p t e", e=E)
        past2 = room(TILES * E).rearrange("p (t e) -> p t e", e=E)
        texp, toff, toff2 = room(TILES), room(TILES), room(TILES)
        texp_i, toff_i = room(TILES, I32), room(TILES, I32)
        base_i = room(E, I32)
        assert taken[0] <= 2 * HALF
        hid_bank, row_bank, y_bank, hidT_bank = bank[1:3], bank[3:5], bank[5:7], bank[0]

        s_w_in = sem("expert_weights_loaded")
        s_b_in = sem("biases_loaded")
        s_b_hi = sem("bias_hi")
        s_b_r1 = sem("bias_rest1")
        s_b_mid = sem("bias_mid")
        s_b_lo = sem("bias_lo")
        s_b_rows = sem("bias_rows_loaded")
        s_plan = sem("plan_steps")
        s_zero = sem("filling_zero")
        s_fill = sem("filling_stored")
        s_tin = [sem(f"tile_loaded{i}") for i in range(4)]
        s_xnb = sem("tile_rows_normal")
        s_xT_ps = sem("tile_transposed_in_psum")
        s_xT = sem("tile_transposed")
        s_h_ps = sem("hidden_in_psum")
        s_h = sem("hidden_ready")
        s_hT_ps = sem("hiddenT_in_psum")
        s_hT = sem("hiddenT_ready")
        s_yt_ps = sem("tile_out_in_psum")
        s_rowi = sem("row_numbers_integer")
        s_yt = sem("tile_out_ready")
        s_out = [sem(f"tile_scattered{i}") for i in range(2)]
        PLAN = 13

        def tiles(eng, step, before):
            for t in range(-before, 4):
                step(t, t % 4)
            with eng.Fori(1, TILES // 4 - 1) as i:
                for c in range(4):
                    step(4 * i + c, c)
            for t in range(TILES - 4, TILES + 2):
                step(t, t % 4)

        def fill_regions(eng, experts):
            eng.wait_ge(s_plan, PLAN)
            for i in experts:
                end = eng.value_load(base_i[0:1, i:i + 1], min_val=i * REGION, max_val=i * REGION + B * N)
                eng.dma_start(regions[bass.ds(end, P), :], fill).then_inc(s_fill, 16)

        def moe_loads(sp):
            sp.wait_ge(s_summed, 32 * (UNITS - 1))
            for i in range(E):
                sp.dma_start(w1_s[:, i, :, :], w1[:, i, :, :]).then_inc(s_w_in, 16)
                sp.dma_start(w2_s[:, i, :, :], w2[:, i, :, :]).then_inc(s_w_in, 16)
            sp.wait_ge(s_summed, 32 * UNITS)
            sp.dma_start(bstage, b12).then_inc(s_b_in, 16)
            sp.wait_ge(s_b_lo, 1)
            for i in range(3):
                sp.dma_start(brows[i:i + 1, :], bsplit[:, i, :]).then_inc(s_b_rows, 16)
            sp.wait_ge(s_zero, 2)
            sp.dma_start(regions[E * REGION:E * REGION + P, :], fill).then_inc(s_fill, 16)
            fill_regions(sp, range(0, E // 2))
            sp.wait_ge(s_fill, 16 * (E + 1))
            sp.wait_ge(s_scat, 16 * UNITS)

            def load(t, c):
                n = t + 3
                if not is_tile(n):
                    return
                at = sp.value_load(toff_i[0:1, bass.ds(n, 1)], min_val=0, max_val=E * REGION)
                wait(sp, s_yt, n - 3)
                take_waits(sp)
                sp.dma_start(tin[:, (c + 3) % 4, :], regions[bass.ds(at, P), :]).then_inc(s_tin[(c + 3) % 4], 16)

            tiles(sp, load, 3)

        def moe_scatter(pool):
            last_row = pool.snap(pool.to_reg(B * N - 1))

            def store(t, c):
                n = t - 1
                if not is_tile(n):
                    return
                par = (c - 1) % 2
                pool.wait_ge(s_yt, n + 1)
                pool.wait_ge(s_rowi, n + 1)
                take_waits(pool)
                nc.gpsimd.indirect_dma_start(
                    out=out_rows, out_offset=bass.IndirectOffsetOnAxis(ap=rowi[:, par:par + 1], axis=0),
                        in_=yout[:, par, :], in_offset=None, bounds_check=last_row, oob_is_err=False
                ).then_inc(s_out[par], 16)

            tiles(pool, store, 0)
            for par in range(2):
                pool.wait_ge(s_out[par], 16 * TILES // 2)

        def moe_gelu(act):
            act.wait_ge(s_summed, 32 * UNITS)
            act.wait_ge(s_zero, 2)
            fill_regions(act, range(E // 2, E))

            def step(t, c):
                par, last = c % 2, (c + 1) % 2
                if is_tile(t - 1):
                    act.wait_ge(s_hT_ps, t)
                    wait(act, s_yt_ps, t - 2)
                    nc.scalar.activation(hidT[:, last, :, :], hidT_bank[:, :].rearrange("p (k n) -> p k n", k=FC),
                                         ACT.Copy).then_inc(s_hT, 1)
                if is_tile(t):
                    act.wait_ge(s_h_ps, t + 1)
                    wait(act, s_hT_ps, t - 1)
                    nc.scalar.activation(hid[:, par, :], hid_bank[par][:, :], ACT.Gelu).then_inc(s_h, 1)

            tiles(act, step, 0)

        def moe_matmuls(pe):
            pe.wait_ge(s_w_in, 16 * 2 * E)
            pe.wait_ge(s_b_rows, 48)
            pe.wait_ge(s_plan, PLAN)
            pe.wait_ge(s_x2, UNITS)
            pe.wait_ge(s_base, UNITS)
            pe.wait_ge(s_ex, UNITS)

            def step(t, c):
                par, last = c % 2, (c + 1) % 2
                if is_tile(t - 1):
                    pe.wait_ge(s_h, t)
                    wait(pe, s_hT, t - 1)
                    for k in range(FC):
                        op = nc.tensor.transpose(hidT_bank[:, k * P:(k + 1) * P], hid[:, last, k * P:(k + 1) * P],
                                                 ident[:])
                    op.then_inc(s_hT_ps, 1)
                if is_tile(t):
                    ex_t = pe.value_load(texp_i[0:1, bass.ds(t, 1)], min_val=0, max_val=E - 1)
                    pe.wait_ge(s_xT, t + 1)
                    wait(pe, s_h, t - 1)
                    nc.tensor.matmul(hid_bank[par][:, :], ones3, brows[:, bass.ds(ex_t * F, F)],
                                     start=True, stop=False)
                    for k in range(KC):
                        op = nc.tensor.matmul(hid_bank[par][:, :], xnbT[:, par, k, :],
                                              flat[:, bass.ds(ex_t * (KC * F) + k * F, F)],
                                              start=False, stop=(k == KC - 1))
                    op.then_inc(s_h_ps, 1)
                if is_tile(t + 1):
                    pe.wait_ge(s_xnb, t + 2)
                    wait(pe, s_xT, t)
                    for k in range(KC):
                        op = nc.tensor.transpose(row_bank[last][:, k * P:(k + 1) * P],
                                                 xnb[:, last, k * P:(k + 1) * P], ident[:])
                    op.then_inc(s_xT_ps, 1)
                if is_tile(t - 1):
                    ex_l = pe.value_load(texp_i[0:1, bass.ds(t - 1, 1)], min_val=0, max_val=E - 1)
                    pe.wait_ge(s_hT, t)
                    wait(pe, s_yt, t - 2)
                    nc.tensor.matmul(y_bank[last][:, 0:C], ones3, brows[:, bass.ds(ex_l * C + E * F, C)],
                                     start=True, stop=False)
                    for k in range(FC):
                        op = nc.tensor.matmul(y_bank[last][:, 0:C], hidT[:, last, k, :],
                                              flat[:, bass.ds(ex_l * (FC * C) + (E * KC * F + k * C), C)],
                                              start=False, stop=(k == FC - 1))
                    op.then_inc(s_yt_ps, 1)

            tiles(pe, step, 1)

        def moe_biases(dve):
            dve.wait_ge(s_summed, 32 * UNITS)
            nc.vector.memset(ones3, 1.0)
            nc.vector.memset(fill, 0.0).then_inc(s_zero, 1)
            dve.wait_ge(s_zero, 1)
            nc.vector.memset(fill[:, AT_ID:AT_ID + 1], NO_ROW).then_inc(s_zero, 1)
            dve.wait_ge(s_b_in, 16)
            nc.vector.tensor_copy(bsplit[:, 0, :], bstage).then_inc(s_b_hi, 1)
            dve.wait_ge(s_b_hi, 1)
            nc.vector.tensor_tensor(brem, bstage, bsplit[:, 0, :], ALU.subtract).then_inc(s_b_r1, 1)
            dve.wait_ge(s_b_r1, 1)
            nc.vector.tensor_copy(bsplit[:, 1, :], brem).then_inc(s_b_mid, 1)
            dve.wait_ge(s_b_mid, 1)
            nc.vector.tensor_tensor(bsplit[:, 2, :], brem, bsplit[:, 1, :], ALU.subtract).then_inc(s_b_lo, 1)


        def moe_vector(dve):
            plan = [0]

            def planned(op):
                plan[0] += 1
                op.then_inc(s_plan, 1)
                dve.wait_ge(s_plan, plan[0])

            dve.wait_ge(s_summed, 32 * UNITS)
            dve.wait_ge(s_base, UNITS)
            planned(nc.vector.tensor_tensor(cnt, base[:], base0, ALU.subtract))
            planned(nc.vector.tensor_tensor(above, cnt.unsqueeze(2).to_broadcast([P, E, UNITS]),
                                            full.unsqueeze(1).to_broadcast([P, E, UNITS]), ALU.is_gt))
            planned(nc.vector.tensor_reduce(ntile, above, AX.X, ALU.add))
            planned(nc.vector.tensor_tensor_scan(tend, tri[:, 1, 0:E], ntile, 0.0, ALU.mult, ALU.add))
            planned(nc.vector.tensor_tensor(past, tend.unsqueeze(1).to_broadcast([P, TILES, E]),
                                            tile_no.unsqueeze(2).to_broadcast([P, TILES, E]), ALU.is_le))
            planned(nc.vector.tensor_reduce(texp, past, AX.X, ALU.add))
            planned(nc.vector.tensor_scalar(tword, ntile, -float(P), float(REGION), ALU.mult, ALU.add))
            planned(nc.vector.tensor_tensor(past2, past, tword.unsqueeze(1).to_broadcast([P, TILES, E]), ALU.mult))
            planned(nc.vector.tensor_reduce(toff, past2, AX.X, ALU.add))
            planned(nc.vector.scalar_tensor_tensor(toff2, tile_no, float(P), toff, ALU.mult, ALU.add))
            planned(nc.vector.tensor_scalar(toff_i, toff2, float(E * REGION), None, ALU.min))
            planned(nc.vector.tensor_scalar(texp_i, texp, float(E - 1), None, ALU.min))
            planned(nc.vector.tensor_copy(base_i, base[:]))
            assert plan[0] == PLAN
            def step(t, c):
                par, last = c % 2, (c + 1) % 2
                if is_tile(t + 1):
                    dve.wait_ge(s_xT_ps, t + 2)
                    wait(dve, s_h_ps, t)
                    nc.vector.tensor_copy(xnbT[:, last, :, :], row_bank[last][:, 0:C].rearrange(
                        "p (k n) -> p k n", k=KC)).then_inc(s_xT, 1)
                if is_tile(t + 2):
                    n, slot4 = t + 2, (c + 2) % 4
                    dve.wait_ge(s_tin[slot4], load_count(n, slot4))
                    wait(dve, s_xT_ps, n - 1)
                    nc.vector.tensor_scalar(xnb[:, par, :], tin[:, slot4, 0:C],
                                            tin[:, slot4, AT_MEAN:AT_MEAN + 1], tin[:, slot4, AT_SCALE:AT_SCALE + 1],
                                            ALU.subtract, ALU.mult).then_inc(s_xnb, 1)
                if is_tile(t - 1):
                    n, slot4 = t - 1, (c + 3) % 4
                    wait(dve, s_out[last], 8 * (n - last))
                    nc.vector.tensor_copy(rowi[:, last:last + 1], tin[:, slot4, AT_ID:AT_ID + 1]).then_inc(s_rowi, 1)
                    dve.wait_ge(s_yt_ps, n + 1)
                    nc.vector.scalar_tensor_tensor(yout[:, last, :], y_bank[last][:, 0:C],
                                                   tin[:, slot4, AT_WEIGHT:AT_WEIGHT + 1], tin[:, slot4, 0:C],
                                                   ALU.mult, ALU.add).then_inc(s_yt, 1)

            tiles(dve, step, 2)

        def load_count(n, slot4):
            return 16 * ((n - slot4) // 4 + 1) if isinstance(n, int) else (n - slot4) * 4 + 16

        @block.sync
        def _(sp):
            for dst, src in consts:
                sp.dma_start(dst, src).then_inc(s_const, 16)

            def slot(v, b, c):
                odd, last = c % 2, (c + 1) % 2
                n = v - 1
                if is_unit(n):
                    wait(sp, s_summed, 32 * (n - 1))
                    take_waits(sp)
                    for part, ready in enumerate((s_hi, s_mid, s_split)):
                        sp.wait_ge(ready, n + 1)
                        take_waits(sp)
                        for g in range(GROUPS):
                            sp.dma_start(g3[32 * part:32 * part + 32, last, g, :],
                                         parts[32 * g:32 * g + 32, part, :]).then_inc(s_g3, 16)
                    wait(sp, s_x1, n - 1)
                    take_waits(sp)
                    sp.dma_start(xres[:, last:last + 1, :], rows[:, bass.ds(n, 1), :]).then_inc(s_res_in, 16)
                if not odd and is_batch(b + 1):
                    wait(sp, s_xnT_ps, b + 1)
                    take_waits(sp)
                    sp.dma_start(xin[:], rows[:, bass.ds(v + 2, 2), :]).then_inc(s_x_in, 16)
                if odd and is_batch(b):
                    wait(sp, s_kv_ps, b)
                    take_waits(sp)
                    sp.dma_start(cT[:], ctxT[:, bass.ds(b, 1), :, :]).then_inc(s_ctx_in, 16)

            sp.dma_start(xin[:], rows[:, 0:2, :]).then_inc(s_x_in, 16)
            slots(sp, slot)
            moe_loads(sp)

        def pair_ap(v_par, j, p):
            return e[:, v_par, j, p, :]

        def query(b_par, u, j, p):
            s = 2 * j + p // GROUPS
            return q2[:, b_par, u, p % GROUPS, s:s + 1]

        def ahead(v, b, c, step, by):
            if step + by < STEPS:
                return v, b, c, step + by
            return v + 1, (b + c % 2), (c + 1) % 4, step + by - STEPS

        def wait_relu(eng, v, b, j):
            if j == 0:
                wait(eng, s_k, b + 1)
                wait(eng, s_q, 2 * (b + 1))
            wait(eng, s_summed, 32 * (v - 2) + 4 * j + 4)

        @block.gpsimd
        def _(pool):
            pool.wait_ge(s_const, 16 * len(consts))
            pool.wait_ge(s_setup, SETUP)

            def slot(v, b, c):
                for step in range(STEPS):
                    if step == 1 and is_unit(v - 1):
                        pool.wait_ge(s_mid, v)
                        nc.gpsimd.tensor_tensor(parts[:, 2, :], rem[:], parts[:, 1, :], ALU.subtract
                                                ).then_inc(s_split, 1)
                    vv, bb, cc, j = ahead(v, b, c, step, RELU_AHEAD)
                    if is_unit(vv):
                        wait_relu(pool, vv, bb, j)
                        take_waits(pool)
                        for p in relu_pairs(v, step)[1]:
                            op = nc.gpsimd.tensor_scalar(
                                pair_ap(cc % 2, j, p), k2[:, cc // 2, :], query(cc // 2, cc % 2, j, p), 0.0,
                                ALU.add, ALU.max)
                        op.then_inc(s_relu_pool, 1)
                    if step == 0 and is_unit(v - 1):
                        wait(pool, s_attT, v - 3)
                        pool.wait_ge(s_hi, v)
                        nc.gpsimd.tensor_tensor(rem[:], ex[:], parts[:, 0, :], ALU.subtract).then_inc(s_r1, 1)
                    if step == 4 and c % 2 == 0 and is_batch(b - 1):
                        wait(pool, s_kT, 2 * b)
                        wait(pool, s_xs_ps, 4 * (v - 2))
                        for k in range(KC):
                            op = nc.gpsimd.tensor_tensor(
                                kbd[:, k, :, :], kT[:, k, :].unsqueeze(1).to_broadcast([P, H // 2, NK]),
                                headmask[:, :].unsqueeze(2).to_broadcast([P, H // 2, NK]), ALU.mult)
                        op.then_inc(s_kbd, 1)
                    if step == 6 and is_unit(v - 3):
                        row = pay[:, 1 - c % 2, :]
                        pool.wait_ge(s_rs3, v - 2)
                        wait(pool, s_xn3T_ps, v - 3)
                        if is_unit(v - 2):
                            pool.wait_ge(s_xn2T_ps, v - 1)
                        take_waits(pool)
                        nc.gpsimd.tensor_scalar(xn3[:], row[:, 0:C], row[:, AT_MEAN:AT_MEAN + 1],
                                                row[:, AT_SCALE:AT_SCALE + 1], ALU.subtract, ALU.mult
                                                ).then_inc(s_xn3, 1)
                    if step == 6 and is_unit(v - 2):
                        pool.wait_ge(s_x1, v - 1)
                        wait(pool, s_x2, v - 2)
                        nc.gpsimd.tensor_tensor(x1b[:], x1[:], xbo_s[:], ALU.add).then_inc(s_x1b, 1)
                    if step == 2 and is_unit(v - 5):
                        row = pay[:, 1 - c % 2, :]
                        wait(pool, s_idn, v - 5)
                        pool.wait_ge(s_x2, v - 4)
                        take_waits(pool)
                        nc.gpsimd.tensor_copy(row[:, AT_ID:AT_ID + 1], row_id).then_inc(s_id, 1)
                        pool.wait_ge(s_id, v - 4)
                        pool.wait_ge(s_wt, v - 4)
                        pool.wait_ge(s_posi, v - 4)
                        take_waits(pool)
                        nc.gpsimd.tensor_scalar(row_id, row_id, float(P), None, ALU.add).then_inc(s_idn, 1)
                        nc.gpsimd.indirect_dma_start(
                            out=regions, out_offset=bass.IndirectOffsetOnAxis(ap=posi[:, 0:1], axis=0),
                            in_=row, in_offset=None).then_inc(s_scat, 16)

            slots(pool, slot)
            moe_scatter(pool)

        @block.scalar
        def _(act):
            act.wait_ge(s_const, 16 * len(consts))
            act.wait_ge(s_setup, SETUP)

            def slot(v, b, c):
                odd, last, pb = c % 2, (c + 1) % 2, c // 2
                for step in range(STEPS):
                    vs, _, cs, js = ahead(v, b, c, step, SQRT_AHEAD)
                    if is_unit(vs):
                        wait(act, s_relu_dve, 8 * vs + js + 1)
                        wait(act, s_relu_pool, 8 * vs + js + 1)
                        wait(act, s_relu_act, 8 * vs + js + 1)
                        ej = e[:, cs % 2, js, :, :]
                        nc.scalar.activation(ej, ej, ACT.Sqrt, bias=eps_rho[:]).then_inc(s_sqrt, 1)
                    background(v, b, c, step)
                    vv, bb, cc, j = ahead(v, b, c, step, RELU_AHEAD)
                    if is_unit(vv):
                        wait_relu(act, vv, bb, j)
                        for p in relu_pairs(v, step)[2]:
                            op = nc.scalar.activation(pair_ap(cc % 2, j, p), k2[:, cc // 2, :], ACT.Relu,
                                                      bias=query(cc // 2, cc % 2, j, p))
                        op.then_inc(s_relu_act, 1)
                    if step == 4 and is_unit(v - 2):
                        act.wait_ge(s_mv2, v - 1)
                        wait(act, s_rs2, v - 2)
                        nc.scalar.activation(sd2[:], mv2[:, 1:2], ACT.Sqrt, bias=eps_ln[:]).then_inc(s_sd2, 1)
                    if step == 5 and is_unit(v - 3):
                        act.wait_ge(s_mv3, v - 2)
                        wait(act, s_rs3, v - 3)
                        nc.scalar.activation(sd3[:], pay[:, 1 - c % 2, AT_SCALE:AT_SCALE + 1], ACT.Sqrt,
                                             bias=eps_ln[:]).then_inc(s_sd3, 1)

            def background(v, b, c, step):
                odd, last, pb = c % 2, (c + 1) % 2, c // 2
                nb = (pb + odd) % 2
                if step == 0:
                    if odd and is_batch(b + 1):
                        act.wait_ge(s_mv1, 2 * (b + 2))
                        wait(act, s_rs1, b + 1)
                        nc.scalar.activation(sd1[:], mv1[:, :, 1], ACT.Sqrt, bias=eps_ln[:]).then_inc(s_sd1, 1)
                    if is_unit(v - 1):
                        act.wait_ge(s_nmax, v)
                        wait(act, s_exT_ps, v - 1)
                        wait(act, s_split, v - 1)
                        nc.scalar.activation(ex[:], score_bank[last], ACT.Exp, bias=nmax[:]).then_inc(s_ex, 1)
                    if is_unit(v - 5):
                        act.wait_ge(s_lsub, v - 4)
                        wait(act, s_wt, v - 5)
                        nc.scalar.activation(els[:], lg[:], ACT.Exp, accum_out=sume[:]).then_inc(s_els, 1)
                    if is_unit(v - 3):
                        act.wait_ge(s_sub, 4 * (v - 2))
                        nc.scalar.activation(pr[:], pr[:], ACT.Exp, scale=D ** -0.5).then_inc(s_pr, 1)
                if step == 1 and is_unit(v - 4):
                    act.wait_ge(s_xn3T_ps, v - 3)
                    wait(act, s_lg_ps, v - 4)
                    nc.scalar.activation(xn3T[:], work2[:, 0:C].rearrange("p (k n) -> p k n", k=KC), ACT.Copy
                                         ).then_inc(s_xn3T, 1)
                if step == 1 and odd and is_batch(b + 1):
                    act.wait_ge(s_xnT_ps, b + 2)
                    wait(act, s_vy_ps, b + 1)
                    nc.scalar.activation(xnT[:], work2[:, :].rearrange("p (k n) -> p k n", k=KC), ACT.Copy
                                         ).then_inc(s_xnT, 1)
                if step in (1, 2) and is_unit(v - 3):
                    for i, bk in ((0, work0), (1, work1)):
                        g = 2 * (step - 1) + i
                        act.wait_ge(s_pT_ps, 4 * (v - 3) + g + 1)
                        wait(act, s_pv_ps, v - 3)
                        nc.scalar.activation(pT[:, 4 * g:4 * g + 4, :],
                                             bk[0:NK, :].rearrange("p (h q) -> p h q", h=4), ACT.Copy
                                             ).then_inc(s_pT, 1)
                if step == 4 and odd and is_batch(b + 1):
                    act.wait_ge(s_k_ps, b + 2)
                    nc.scalar.activation(k2[:, nb, :], work2[:, 0:N], ACT.Copy).then_inc(s_k, 1)
                if step == 5:
                    if is_unit(v - 1):
                        act.wait_ge(s_exT_ps, v)
                        wait(act, s_o_ps, v - 1)
                        nc.scalar.activation(exT[:], exT_ps.rearrange("p (k n) -> p k n", k=2), ACT.Copy
                                             ).then_inc(s_exT, 1)
                    if is_unit(v - 2):
                        act.wait_ge(s_xn2T_ps, v - 1)
                        wait(act, s_qT_ps, v - 2)
                        nc.scalar.activation(xn2T[:], xn2T_ps.rearrange("p (k n) -> p k n", k=KC), ACT.Copy
                                             ).then_inc(s_xn2T, 1)
                if step == 6 and is_unit(v - 2):
                    act.wait_ge(s_qT_ps, v - 1)
                    wait(act, s_xs_ps, 4 * (v - 2))
                    for k in range(KC):
                        nc.scalar.activation(qT[:, k, :], qT_ps[:, k * P:(k + 1) * P], ACT.Identity,
                                             bias=xbq_s[:, k:k + 1]).then_inc(s_qT, 1)

            slots(act, slot)
            moe_gelu(act)

        @block.tensor
        def _(pe):
            pe.wait_ge(s_const, 16 * len(consts))
            pe.wait_ge(s_setup, SETUP - 2)
            nc.tensor.matmul(work0[:, 0:C], minus_rho[:], we_s[0:A, 0:C], start=True, stop=True).then_inc(s_vb_ps, 1)
            pe.wait_ge(s_setup, SETUP)

            def scores(v, c, step, first):
                for p in range(first, first + GROUPS):
                    g, s = p % GROUPS, 2 * step + p // GROUPS
                    op = nc.tensor.matmul(score_bank[c % 2][32 * g:32 * g + 32, :], selw[:, s, :],
                                          e[:, c % 2, step, p, :], start=(s == 0), stop=(s == SIDE - 1),
                                          tile_position=(0, 32 * g))
                if step == STEPS - 1 and first:
                    op.then_inc(s_scores, 1)

            def spread(n, par, j, m):
                s, g = 2 * j + m // 2, 2 * (m % 2)
                wait(pe, s_summed, 32 * n + 4 * j + m - 3)
                nc.tensor.matmul(weight_bank[m][:, :], selb[:, s, :], g3[:, par, g:g + 2, :],
                                 start=True, stop=True).then_inc(s_wb, 1)

            def slot(v, b, c):
                odd, last = c % 2, (c + 1) % 2
                for step in range(STEPS):
                    n, par, j = (v - 1, last, step - LAG) if step >= LAG else (v - 2, odd, step + STEPS - LAG)
                    if is_unit(n) and j == 0:
                        pe.wait_ge(s_g3, 192 * (n + 1))
                    for m in range(4):
                        if is_unit(n):
                            spread(n, par, j, m)
                        if is_unit(v) and step == 1 and m == 0:
                            pe.wait_ge(s_sqrt, 8 * v + 1)
                            wait(pe, s_ex, v)
                            scores(v, c, 0, 0)
                            scores(v, c, 0, GROUPS)
                        if is_unit(v) and step == 1 and m == 2:
                            pe.wait_ge(s_sqrt, 8 * v + 2)
                            scores(v, c, 1, 0)
                            scores(v, c, 1, GROUPS)
                        if is_unit(v) and step > 1 and m % 2 == 0:
                            if m == 0:
                                pe.wait_ge(s_sqrt, 8 * v + step + 1)
                            scores(v, c, step, 2 * m)
                    for m in range(4):
                        if m == 3:
                            self_attention(v, b, c, step)
                        cross(v, b, c, step, m)

            def self_attention(v, b, c, step):
                odd, last, pb = c % 2, (c + 1) % 2, c // 2
                if odd and is_batch(b + 1):
                    if step == 1:
                        pe.wait_ge(s_xn1, 2 * (b + 2))
                        wait(pe, s_exT, v - 1)
                        wait(pe, s_vy, b + 1)
                        wait(pe, s_sub, 4 * (v - 2))
                        wait(pe, s_xn3T, v - 3)
                        for r in range(2):
                            for k in range(KC):
                                op = nc.tensor.transpose(work2[:, k * N + r * P:k * N + r * P + P],
                                                         xin[:, r, k * P:(k + 1) * P], ident[:])
                        op.then_inc(s_xnT_ps, 1)
                    if step == 2:
                        pe.wait_ge(s_xnT, b + 2)
                        for k in range(KC):
                            op = nc.tensor.matmul(work2[:, 0:N], wq_s[:, k, :], xnT[:, k, :],
                                                  start=(k == 0), stop=(k == KC - 1))
                        op.then_inc(s_q_ps, 1)
                    if step == 3:
                        pe.wait_ge(s_q, 2 * (b + 2))
                        for k in range(KC):
                            op = nc.tensor.matmul(work2[:, 0:N], wk_s[:, k, :], xnT[:, k, :],
                                                  start=(k == 0), stop=(k == KC - 1))
                        op.then_inc(s_k_ps, 1)
                    if step == 5:
                        pe.wait_ge(s_k, b + 2)
                        if is_unit(v - 1):
                            pe.wait_ge(s_exT, v)
                        for r in range(2):
                            for k in range(KC):
                                op = nc.tensor.matmul(work2[:, r * C:(r + 1) * C], xnT[:, k, r * P:(r + 1) * P],
                                                      wy_s[:, k, :], start=(k == 0), stop=(k == KC - 1))
                        op.then_inc(s_vy_ps, 1)
                if step == 0 and is_unit(v - 4):
                    pe.wait_ge(s_xn3, v - 3)
                    if is_unit(v - 3):
                        pe.wait_ge(s_sub, 4 * (v - 3) + 2)
                    for k in range(KC):
                        op = nc.tensor.transpose(work2[:, k * P:(k + 1) * P], xn3[:, k * P:(k + 1) * P], ident[:])
                    op.then_inc(s_xn3T_ps, 1)
                if step == 2 and not odd and is_batch(b - 1):
                    pe.wait_ge(s_ctx_in, 16 * b)
                    pe.wait_ge(s_exT, v - 1)
                    wait(pe, s_xn3T, v - 3)
                    if is_batch(b):
                        pe.wait_ge(s_vy, b + 1)
                    for k in range(KC):
                        for h in range(2):
                            nc.tensor.matmul(k_ctx_ps[:, k * NK:(k + 1) * NK], xwk_s[:, h, k * P:(k + 1) * P],
                                             cT[:, h, :], start=(h == 0), stop=(h == 1))
                    for h in range(2):
                        op = nc.tensor.matmul(v_ctx_ps, cT[:, h, :], xwv_s[:, h, :],
                                              start=(h == 0), stop=(h == 1))
                    op.then_inc(s_kv_ps, 1)
                if step == 3 and is_unit(v - 2):
                    pe.wait_ge(s_ew2, 2 * (v - 1))
                    pe.wait_ge(s_exT, v - 1)
                    pe.wait_ge(s_vy, b)
                    vb = (pb + 1) % 2
                    for r in range(2):
                        nc.tensor.matmul(out_ps, exT[:, r, :], vy[:, vb, r, :],
                                         start=(r == 0), stop=False)
                    nc.tensor.matmul(out_ps, ew2[:].rearrange("p g i s -> p (g i s)"), we_s[:],
                                     start=False, stop=True).then_inc(s_o_ps, 1)
                if step == 4 and is_unit(v - 1):
                    pe.wait_ge(s_ex, v)
                    if odd and is_batch(b + 1):
                        pe.wait_ge(s_k, b + 2)
                    if not odd:
                        if is_batch(b - 1):
                            pe.wait_ge(s_kT, 2 * b)
                            pe.wait_ge(s_vx, b)
                        if is_batch(b):
                            pe.wait_ge(s_vy, b + 1)
                    for r in range(2):
                        op = nc.tensor.transpose(exT_ps[:, r * P:(r + 1) * P], ex[:, r * P:(r + 1) * P], ident[:])
                    op.then_inc(s_exT_ps, 1)

            def head_scores(n, g, bk):
                k, h = g // 2, 4 * (g % 2)
                nc.tensor.matmul(bk[:, 0:4 * NK], qT[:, k, :], kbd[:, k, h:h + 4, :], start=True, stop=True
                                 ).then_inc(s_xs_ps, 1)

            def cross(v, b, c, step, m):
                n, late = v - 2, v - 3
                if step == 7 and is_unit(n):
                    if m == 1:
                        pe.wait_ge(s_qT, 2 * (n + 1))
                        pe.wait_ge(s_kbd, b)
                        head_scores(n, 0, work1)
                        wait(pe, s_exT, n + 2 if is_unit(n + 1) else n + 1)
                        if c % 2 == 1 and is_batch(b + 1):
                            pe.wait_ge(s_vy, b + 2)
                        head_scores(n, 1, work2)
                    if m == 2:
                        wait(pe, s_x2, late + 1)
                        if is_unit(v - 4):
                            pe.wait_ge(s_base, v - 3)
                            pe.wait_ge(s_rank, v - 3)
                        head_scores(n, 2, work0)
                    if m == 3:
                        pe.wait_ge(s_sub, 4 * n + 1)
                        head_scores(n, 3, work1)
                if step in (1, 2) and m in (1, 2) and is_unit(late):
                    i = m - 1
                    g = 2 * (step - 1) + i
                    bk = (work0, work1)[i]
                    pe.wait_ge(s_pr, late + 1)
                    if step == 2:
                        pe.wait_ge(s_pT, 4 * late + g - 1)
                    for h in range(4):
                        op = nc.tensor.transpose(bk[0:NK, h * P:(h + 1) * P], pr[:, 4 * g + h, :], ident[:])
                    op.then_inc(s_pT_ps, 1)
                if step == 3 and m == 0 and is_unit(late):
                    pe.wait_ge(s_pT, 4 * (late + 1))
                    pe.wait_ge(s_vx, b if c % 2 else b - 1)
                    for dens in range(2):
                        for k in range(KC):
                            for i in range(2):
                                for g in range(GROUPS):
                                    pair = GROUPS * k + g
                                    op = nc.tensor.matmul(
                                        work0[32 * g:32 * g + 32, C * dens + P * k:C * dens + P * k + P],
                                        vones[:, i, :] if dens else vx[:, pair, i, :], pT[:, 2 * pair + i, :],
                                        start=(i == 0), stop=(i == 1), tile_position=(0, 32 * g))
                    op.then_inc(s_pv_ps, 1)
                if step == 3 and m == 2 and is_unit(v - 4):
                    pe.wait_ge(s_xn3T, v - 3)
                    for k in range(KC):
                        op = nc.tensor.matmul(logit_ps, xn3T[:, k, :], wr_s[:, k, :],
                                              start=(k == 0), stop=(k == KC - 1))
                    op.then_inc(s_lg_ps, 1)
                if step == 5 and m == 0 and is_unit(late):
                    pe.wait_ge(s_attT, late + 1)
                    for k in range(KC):
                        op = nc.tensor.matmul(y_ps, attT[:, k, :], xwo_s[:, k, :],
                                              start=(k == 0), stop=(k == KC - 1))
                    op.then_inc(s_y_ps, 1)
                if step == 5 and m == 1 and is_unit(n):
                    pe.wait_ge(s_xn2, n + 1)
                    if is_unit(v - 4):
                        pe.wait_ge(s_lg, v - 3)
                    for k in range(KC):
                        op = nc.tensor.transpose(xn2T_ps[:, k * P:(k + 1) * P], xn2[:, k * P:(k + 1) * P], ident[:])
                    op.then_inc(s_xn2T_ps, 1)
                if step == 6 and m == 2 and is_unit(v - 4):
                    pe.wait_ge(s_oh, v - 3)
                    if is_unit(late):
                        pe.wait_ge(s_x2, late + 1)
                    for i in range(2):
                        op = nc.tensor.matmul(rank_ps[:, E * i:E * i + E], tri[:, i, :], oh[:], start=True, stop=True)
                    op.then_inc(s_rank_ps, 1)
                if step == 6 and m == 1 and is_unit(n):
                    pe.wait_ge(s_xn2T, n + 1)
                    for i in range(2):
                        for k in range(KC):
                            op = nc.tensor.matmul(qT_ps[:, i * P:(i + 1) * P], xwq_s[:, k, i * P:(i + 1) * P],
                                                  xn2T[:, k, :], start=(k == 0), stop=(k == KC - 1))
                    op.then_inc(s_qT_ps, 1)

            slots(pe, slot)
            moe_matmuls(pe)

        @block.vector
        def _(dve):
            nc.vector.memset(eps_rho[:], EPS_RHO).then_inc(s_setup, 1)
            nc.vector.memset(eps_ln[:], EPS_LN).then_inc(s_setup, 1)
            nc.vector.memset(minus_rho[:], -(EPS_RHO ** 0.5)).then_inc(s_setup, 1)
            nc.vector.memset(vy[:, :, :, C:C + 1], 1.0).then_inc(s_setup, 1)
            nc.vector.memset(vx[:], 0.0).then_inc(s_setup, 1)
            nc.vector.memset(vones[:], 0.0).then_inc(s_setup, 1)
            dve.wait_ge(s_setup, 6)
            nc.vector.memset(own_half(vones[:].unsqueeze(1)), 1.0).then_inc(s_setup, 1)
            nc.vector.memset(we_s[:, C:C + 1], 0.0).then_inc(s_setup, 1)
            nc.vector.memset(ew2[:], 0.0).then_inc(s_setup, 1)
            dve.wait_ge(s_const, 16 * len(consts))
            nc.vector.tensor_scalar(selw[:].rearrange("p s m -> p (s m)"), stage[:, 0:512], phi[:], None, ALU.mult
                                    ).then_inc(s_setup, 1)
            nc.vector.tensor_copy(selb[:].rearrange("p s m -> p (s m)"), stage[0:96, 512:2560]).then_inc(s_setup, 1)
            nc.vector.tensor_copy(base[:], base0).then_inc(s_setup, 1)
            dve.wait_ge(s_vb_ps, 1)
            nc.vector.tensor_tensor(vbias[:], work0[:, 0:C], stage[:, 2560:2816], ALU.add).then_inc(s_setup, 1)
            dve.wait_ge(s_setup, SETUP - 1)
            nc.vector.tensor_tensor(vbias[:], vbias[:], stage[:, 2816:3072], ALU.add).then_inc(s_setup, 1)
            dve.wait_ge(s_setup, SETUP)

            def ln1_stats(b):
                dve.wait_ge(s_x_in, 16 * (b + 1))
                wait(dve, s_mv1, 2 * b)
                wait(dve, s_xn1, 2 * b)
                for r in range(2):
                    nc.vector.bn_stats(st1[:, r, :], xin[:, r, :]).then_inc(s_st1, 1)
                dve.wait_ge(s_st1, 2 * (b + 1))
                take_waits(dve)
                for r in range(2):
                    nc.vector.bn_aggr(mv1[:, r, :], st1[:, r, :]).then_inc(s_mv1, 1)

            def weigh(n, par, j, p):
                s, g = 2 * j + p // 4, p % 4
                if p % 2 == 0:
                    dve.wait_ge(s_wb, 32 * n + 4 * j + p // 2 + 1)
                ep = pair_ap(par, j, p)
                op = nc.vector.tensor_tensor_reduce(
                    out=ep, in0=ep, in1=weight_bank[p // 2][:, (p % 2) * N:(p % 2) * N + N], scale=1.0,
                    scalar=0.0, op0=ALU.mult, op1=ALU.add, accum_out=ew[:, par, g, s:s + 1])
                if p % 2 == 1:
                    op.then_inc(s_summed, 1)

            def slot(v, b, c):
                odd, last = c % 2, (c + 1) % 2
                for step in range(STEPS):
                    n, par, j = (v - 1, last, step - LAG) if step >= LAG else (v - 2, odd, step + STEPS - LAG)
                    vv, bb, cc, jj = ahead(v, b, c, step, RELU_AHEAD)
                    mine = relu_pairs(v, step)[0]
                    if is_unit(vv):
                        wait_relu(dve, vv, bb, jj)
                    if is_unit(n) and j == 0:
                        wait(dve, s_ew2, 2 * (n - 1))
                    for p in range(CHUNK):
                        if is_unit(n):
                            weigh(n, par, j, p)
                        if is_unit(vv) and p in mine:
                            op = nc.vector.tensor_scalar(
                                pair_ap(cc % 2, jj, p), k2[:, cc // 2, :], query(cc // 2, cc % 2, jj, p), 0.0,
                                ALU.add, ALU.max)
                            if p == mine[-1]:
                                op.then_inc(s_relu_dve, 1)
                        if step in (0, 1, 2, 3):
                            softmax(v, b, c, step, p)
                        if step in (3, 4, 5):
                            residual(v, b, c, step, p)
                        cross(v, b, c, step, p)
                        routing(v, b, c, step, p)
                        if step == 7 and p == 7 and is_unit(v):
                            dve.wait_ge(s_scores, v + 1)
                            wait(dve, s_ex, v)
                            nc.vector.tensor_reduce(nmax[:], score_bank[odd], AX.X, ALU.max, negate=True
                                                    ).then_inc(s_nmax, 1)
                        if step == 7 and not odd and p == 1 and is_batch(b + 1):
                            ln1_stats(b + 1)

                    if isinstance(v, int) and v == UNITS + 2 and step == 0:
                        moe_biases(dve)

            def softmax(v, b, c, step, p):
                odd, last, pb = c % 2, (c + 1) % 2, c // 2
                nb = (pb + 1) % 2
                n = v - 1
                if is_unit(n):
                    if step == 0 and p == 1:
                        dve.wait_ge(s_ex, v)
                        wait(dve, s_g3, 192 * n)
                        nc.vector.tensor_copy(parts[:, 0, :], ex[:]).then_inc(s_hi, 1)
                    if step == 0 and p == 6:
                        dve.wait_ge(s_r1, v)
                        nc.vector.tensor_copy(parts[:, 1, :], rem[:]).then_inc(s_mid, 1)
                if odd and is_batch(b + 1):
                    if step == 0 and p == 2:
                        dve.wait_ge(s_sd1, b + 2)
                        nc.vector.reciprocal(rs1[:], sd1[:]).then_inc(s_rs1, 1)
                    if step == 0 and p == 3:
                        dve.wait_ge(s_rs1, b + 2)
                        for r in range(2):
                            nc.vector.tensor_scalar(xin[:, r, :], xin[:, r, :], mv1[:, r, 0:1], rs1[:, r:r + 1],
                                                    ALU.subtract, ALU.mult).then_inc(s_xn1, 1)
                if step == 3 and p == 0 and is_unit(v - 2):
                    dve.wait_ge(s_summed, 32 * (v - 1))
                    wait(dve, s_o_ps, v - 2)
                    for i in range(2):
                        half = slice(A * i, A * i + A)
                        nc.vector.tensor_copy(ew2[half, :, i, :], ew[half, odd, :, :]).then_inc(s_ew2, 1)

            def residual(v, b, c, step, p):
                odd, pb = c % 2, c // 2
                nb = (pb + 1) % 2
                n = v - 2
                if is_unit(n):
                    if step == 4 and p == 0:
                        dve.wait_ge(s_o_ps, n + 1)
                        wait(dve, s_rden, n)
                        nc.vector.tensor_scalar(den[:], out_ps[:, C:C + 1], EPS_DEN, None, ALU.add).then_inc(s_den, 1)
                    if step == 4 and p == 1:
                        dve.wait_ge(s_den, n + 1)
                        wait(dve, s_x1, n)
                        nc.vector.reciprocal(rden[:], den[:]).then_inc(s_rden, 1)
                    if step == 4 and p == 2:
                        dve.wait_ge(s_rden, n + 1)
                        dve.wait_ge(s_res_in, 16 * (n + 1))
                        wait(dve, s_x1b, n)
                        wait(dve, s_xn2, n)
                        nc.vector.scalar_tensor_tensor(x1[:], out_ps[:, 0:C], rden[:], xres[:, odd, :],
                                                       ALU.mult, ALU.add).then_inc(s_x1, 1)
                    if step == 4 and p == 3:
                        dve.wait_ge(s_x1, n + 1)
                        wait(dve, s_mv2, n)
                        nc.vector.bn_stats(st2[:], x1[:]).then_inc(s_st2, 1)
                    if step == 4 and p == 4:
                        dve.wait_ge(s_st2, n + 1)
                        take_waits(dve)
                        nc.vector.bn_aggr(mv2[:], st2[:]).then_inc(s_mv2, 1)
                    if step == 5 and p == 0:
                        dve.wait_ge(s_sd2, n + 1)
                        nc.vector.reciprocal(rs2[:], sd2[:]).then_inc(s_rs2, 1)
                    if step == 5 and p == 1:
                        dve.wait_ge(s_rs2, n + 1)
                        wait(dve, s_xn2T_ps, n)
                        wait(dve, s_xn3T_ps, v - 3)
                        nc.vector.tensor_scalar(xn2[:], x1[:], mv2[:, 0:1], rs2[:], ALU.subtract, ALU.mult
                                                ).then_inc(s_xn2, 1)
                if odd and is_batch(b + 1):
                    if step == 3 and p == 1:
                        dve.wait_ge(s_q_ps, b + 2)
                        wait(dve, s_relu_act, 8 * (v - 1))
                        wait(dve, s_relu_pool, 8 * (v - 1))
                        wait(dve, s_relu_dve, 8 * (v - 1))
                        for i in range(2):
                            half = slice(A * i, A * i + A)
                            nc.vector.tensor_copy(
                                q2[half, nb, :, :, :].rearrange("p u g s -> p (u g) s"),
                                work2[half, 0:N].rearrange("p (w i s) -> p w i s", i=2, s=SIDE)[:, :, i, :]
                            ).then_inc(s_q, 1)
                if step == 3 and p == 4 and not odd and is_batch(b - 1):
                    dve.wait_ge(s_kv_ps, b)
                    wait(dve, s_kbd, b - 1)
                    for k in range(KC):
                        nc.vector.tensor_scalar(kT[:, k, :], k_ctx_ps[:, k * NK:(k + 1) * NK], xbk_s[:, k:k + 1],
                                                None, ALU.add).then_inc(s_kT, 1)
                if step == 3 and p == 7 and not odd and is_batch(b - 1):
                    wait(dve, s_pv_ps, v - 2)
                    dve.wait_ge(s_kv_ps, b)
                    nc.vector.tensor_tensor(own_half(vx[:]), v_ctx_ps.rearrange("p (g i d) -> p g i d", i=2, d=D),
                                            xbv_s[:].rearrange("p (g i d) -> p g i d", i=2, d=D), ALU.add).then_inc(s_vx, 1)

            def routing(v, b, c, step, p):
                odd = c % 2
                n, z, w = v - 3, v - 4, v - 5
                if is_unit(n):
                    row = pay[:, 1 - odd, :]
                    if step == 5 and p == 5:
                        dve.wait_ge(s_x2, n + 1)
                        wait(dve, s_mv3, n)
                        nc.vector.bn_stats(st3[:], row[:, 0:C]).then_inc(s_st3, 1)
                    if step == 5 and p == 7:
                        dve.wait_ge(s_st3, n + 1)
                        take_waits(dve)
                        nc.vector.bn_aggr(row[:, AT_MEAN:AT_SCALE + 1], st3[:]).then_inc(s_mv3, 1)
                    if step == 6 and p == 4:
                        dve.wait_ge(s_sd3, n + 1)
                        nc.vector.reciprocal(row[:, AT_SCALE:AT_SCALE + 1], sd3[:]).then_inc(s_rs3, 1)
                if is_unit(z):
                    if step == 4 and p == 4:
                        dve.wait_ge(s_lg_ps, z + 1)
                        if is_unit(v - 2):
                            dve.wait_ge(s_o_ps, v - 1)
                        wait(dve, s_els, z)
                        nc.vector.tensor_tensor(lg[:], logit_ps, br_s[:], ALU.add).then_inc(s_lg, 1)
                    if step == 4 and p == 5:
                        dve.wait_ge(s_lg, z + 1)
                        wait(dve, s_lsub, z)
                        nc.vector.tensor_reduce(nlmax[:], lg[:], AX.X, ALU.max, negate=True).then_inc(s_lmax, 1)
                    if step == 4 and p == 6:
                        dve.wait_ge(s_lmax, z + 1)
                        nc.vector.tensor_scalar(lg[:], lg[:], nlmax[:], None, ALU.add).then_inc(s_lsub, 1)
                    if step == 5 and p == 2:
                        dve.wait_ge(s_lsub, z + 1)
                        wait(dve, s_oh, z)
                        nc.vector.scalar_tensor_tensor(key[:], lg[:], 0.0, tie, ALU.is_ge, ALU.mult
                                                       ).then_inc(s_key, 1)
                    if step == 5 and p == 3:
                        dve.wait_ge(s_key, z + 1)
                        nc.vector.tensor_reduce(kmax[:], key[:], AX.X, ALU.max).then_inc(s_kmax, 1)
                    if step == 5 and p == 4:
                        dve.wait_ge(s_kmax, z + 1)
                        wait(dve, s_pos, z)
                        wait(dve, s_rank_ps, z)
                        nc.vector.tensor_scalar(oh[:], key[:], kmax[:], None, ALU.is_equal).then_inc(s_oh, 1)
                    if step == 6 and p == 6:
                        dve.wait_ge(s_rank_ps, z + 1)
                        wait(dve, s_base, z)
                        nc.vector.tensor_tensor(rank[:], rank_ps[:, 0:E], base[:], ALU.add).then_inc(s_rank, 1)
                    if step == 6 and p == 7:
                        dve.wait_ge(s_rank, z + 1)
                        nc.vector.tensor_tensor(base[:], rank_ps[:, E:2 * E], base[:], ALU.add).then_inc(s_base, 1)
                    if step == 7 and p == 7:
                        wait(dve, s_posi, z)
                        nc.vector.tensor_tensor_reduce(out=rank[:], in0=oh[:], in1=rank[:], scale=1.0, scalar=0.0,
                                                       op0=ALU.mult, op1=ALU.add, accum_out=pos[:]
                                                       ).then_inc(s_pos, 1)
                if is_unit(w):
                    if step == 1 and p == 3:
                        dve.wait_ge(s_els, w + 1)
                        nc.vector.reciprocal(pay[:, 1 - odd, AT_WEIGHT:AT_WEIGHT + 1], sume[:]).then_inc(s_wt, 1)
                    if step == 1 and p == 4:
                        dve.wait_ge(s_pos, w + 1)
                        wait(dve, s_scat, 16 * w)
                        nc.vector.tensor_copy(posi[:], pos[:]).then_inc(s_posi, 1)

            def cross(v, b, c, step, p):
                odd, pb = c % 2, c // 2
                nb = (pb + 1) % 2
                n, late = v - 2, v - 3
                if step == 6 and p == 1 and odd and is_batch(b + 1):
                    dve.wait_ge(s_vy_ps, b + 2)
                    wait(dve, s_o_ps, v - 1)
                    nc.vector.tensor_tensor(vy[:, nb, :, 0:C], work2[:, :].rearrange("p (r c) -> p r c", r=2),
                                            vbias[:].unsqueeze(1).to_broadcast([P, 2, C]), ALU.add).then_inc(s_vy, 1)
                if is_unit(late):
                    if step == 3 and p == 7:
                        dve.wait_ge(s_pv_ps, late + 1)
                        wait(dve, s_attT, late)
                        if is_unit(v - 1):
                            wait(dve, s_split, v)
                        nc.vector.reciprocal(rhden[:], work0[:, C:2 * C]).then_inc(s_hden, 1)
                    if step == 4 and p == 0:
                        dve.wait_ge(s_hden, late + 1)
                        wait(dve, s_y_ps, late)
                        nc.vector.tensor_tensor(attT[:].rearrange("p k q -> p (k q)"), work0[:, 0:C], rhden[:],
                                                ALU.mult).then_inc(s_attT, 1)
                    if step == 5 and p == 4:
                        dve.wait_ge(s_y_ps, late + 1)
                        dve.wait_ge(s_x1b, late + 1)
                        wait(dve, s_scat, 16 * (late - 1))
                        nc.vector.tensor_tensor(pay[:, 1 - odd, 0:C], y_ps, x1b[:], ALU.add).then_inc(s_x2, 1)
                if step == 7 and is_unit(n):
                    def head_bank(g):
                        return (work1, work2, work0, work1)[g][:, 0:4 * NK].rearrange("p (h k) -> p h k", h=4)

                    if p in HEADS_AT:
                        g = HEADS_AT.index(p)
                        dve.wait_ge(s_xs_ps, 4 * n + g + 1)
                        wait(dve, s_sub, 4 * n)
                        nc.vector.tensor_reduce(hmax[:, 4 * g:4 * g + 4], head_bank(g), AX.X, ALU.max
                                                ).then_inc(s_hmax, 1)
                    if p - 1 in HEADS_AT:
                        g = HEADS_AT.index(p - 1)
                        dve.wait_ge(s_hmax, 4 * n + g + 1)
                        wait(dve, s_pT_ps, 4 * n)
                        nc.vector.tensor_tensor(pr[:, 4 * g:4 * g + 4, :], head_bank(g),
                                                hmax[:, 4 * g:4 * g + 4].unsqueeze(2).to_broadcast([P, 4, NK]),
                                                ALU.subtract).then_inc(s_sub, 1)

            ln1_stats(0)
            slots(dve, slot)
            moe_vector(dve)


def kernel(x, ctx_768, L0_attn_Wq, L0_attn_Wk, L0_attn_Wphi, L0_attn_Wy_w, L0_attn_Wy_b, L0_attn_We_w, L0_attn_We_b,
           L0_xattn_Wq, L0_xattn_bq, L0_xattn_Wk, L0_xattn_bk, L0_xattn_Wv, L0_xattn_bv, L0_xattn_Wo, L0_xattn_bo,
           L0_ffn_Wr, L0_ffn_br, L0_ffn_W1, L0_ffn_b1, L0_ffn_W2, L0_ffn_b2):
    import numpy as np
    import concourse.bacc as bacc
    from concourse import mybir as mb
    from concourse.bass_utils import run_bass_kernel_spmd as run

    def chunks(w, p):
        w = np.asarray(w)
        return w.reshape(w.shape[0] // p, p, -1).transpose(1, 0, 2)

    def rows(w, n):
        return np.tile(np.asarray(w).reshape(1, -1), (n, 1))

    m, s = np.arange(32), np.arange(16)
    half = np.arange(P) // A
    selw = (m[None, None, :] == 16 * half[:, None, None] + s[None, :, None]).astype(np.float32)
    k = np.arange(96) % 32
    selb = (k[:, None, None] == 16 * half[None, None, :] + s[None, :, None]).astype(np.float32)
    headmask = (np.arange(P)[:, None] // 16 == np.arange(8)[None, :]).astype(np.float32)
    route = np.concatenate([rows(np.arange(E, 0, -1), P), rows(REGION * np.arange(E), P),
                            rows(P * np.arange(UNITS), P), rows(np.arange(TILES), P),
                            np.arange(P)[:, None]], 1).astype(np.float32)
    arrays = {
        "x": np.asarray(x),
        "ctxT": np.asarray(ctx_768).transpose(2, 0, 1).reshape(2, CC, B, NK).transpose(1, 2, 0, 3),
        "wq": chunks(np.asarray(L0_attn_Wq).T, P), "wk": chunks(np.asarray(L0_attn_Wk).T, P),
        "wphi": np.asarray(L0_attn_Wphi).reshape(A, 1),
        "wy": chunks(np.asarray(L0_attn_Wy_w).T, P), "wy_b": rows(L0_attn_Wy_b, P),
        "we": np.asarray(L0_attn_We_w).T, "we_b": rows(L0_attn_We_b, P),
        "xwq": chunks(L0_xattn_Wq, P), "xbq": np.asarray(L0_xattn_bq).reshape(KC, P).T,
        "xwk": chunks(L0_xattn_Wk, CC), "xbk": np.asarray(L0_xattn_bk).reshape(KC, P).T,
        "xwv": chunks(L0_xattn_Wv, CC), "xbv": rows(L0_xattn_bv, NK),
        "xwo": chunks(L0_xattn_Wo, P), "xbo": rows(L0_xattn_bo, P),
        "wr": chunks(L0_ffn_Wr, P), "br": rows(L0_ffn_br, P),
        "w1": np.asarray(L0_ffn_W1).reshape(E, KC, P, F).transpose(2, 0, 1, 3),
        "w2": np.asarray(L0_ffn_W2).reshape(E, F // P, P, C).transpose(2, 0, 1, 3),
        "b12": np.concatenate([np.asarray(L0_ffn_b1).ravel(), np.asarray(L0_ffn_b2).ravel()]).reshape(P, -1),
        "ident": np.eye(P, dtype=np.float32),
        "tri": np.stack([np.triu(np.ones((P, P), np.float32), 1), np.ones((P, P), np.float32)], 1),
        "selw": selw.reshape(P, 512), "selb": selb.reshape(96, 2048),
        "headmask": headmask, "route": route,
    }
    arrays = {f"in_{k}": np.ascontiguousarray(v) for k, v in arrays.items()}
    nc = bacc.Bacc("TRN2", target_bir_lowering=False, num_devices=1)
    args = [nc.dram_tensor(k, v.shape, mb.dt.from_np(v.dtype), kind="ExternalInput").ap() for k, v in arrays.items()]
    args.append(nc.dram_tensor("out", (B, N, C), mb.dt.float32, kind="ExternalOutput").ap())
    decoder_args = dict(zip(["x", "ctxT", "wq", "wk", "wphi", "wy", "wy_b", "we", "we_b", "xwq", "xbq", "xwk", "xbk",
                             "xwv", "xbv", "xwo", "xbo", "wr", "br", "w1", "w2", "b12", "ident_h", "tri_h", "selw_h",
                             "selb_h", "headmask_h", "route_h", "out"], args))
    decoder(nc, **decoder_args)
    return run(nc, [arrays], core_ids=[0]).results[0]["out"]
```
